# Optimizing a Trainium2 kernel written in Bass

```python
import numpy as np
import jax
import jax.numpy as jnp

def _softmax(x, axis=-1):
    return jax.nn.softmax(x, axis=axis)

def _gelu(x):
    return jax.nn.gelu(x, approximate=True)

def _silu(x):
    return jax.nn.silu(x)

def _sigmoid(x):
    return jax.nn.sigmoid(x)

def _layernorm(x, axis=-1, eps=1e-05):
    m = jnp.mean(x, axis=axis, keepdims=True)
    v = jnp.var(x, axis=axis, keepdims=True)
    return (x - m) / jnp.sqrt(v + eps)

def _scatter_add(tgt, idx, src, axis=0):
    return tgt.at[idx].add(src)

def _segment_sum(src, seg, n):
    return jax.ops.segment_sum(src, seg, n)
kernel_name = 'mk_seq_preln_d2_jaxref_r8_8c0eea'

def setup_inputs(seed: int=0):
    np.random.seed(seed)
    _w = jnp.asarray

    def _L0_attn_setup():
        import jax, jax.numpy as jnp
        import numpy as np
        from math import sqrt
        N_HEAD = 16
        W_SCALE = 0.02

        def _reference_tuple_inner(x, W_dq, W_uq, W_dkv, W_uk, W_uv, W_o):
            B, T, C = x.shape
            nh = N_HEAD
            hs = C // nh
            n_kvl = W_dkv.shape[0]
            k_eff = (W_dq.T @ W_uq.T @ W_uk).reshape(nh, hs, n_kvl)
            v_eff = jnp.transpose((W_uv.T @ W_o.T).reshape(n_kvl, nh, hs), (1, 0, 2))
            c_kv = x @ W_dkv.T
            q = x @ W_dq.T @ W_uq.T
            q = q.reshape(B, T, nh, hs)
            q_lat = jnp.einsum('bqhd,hdl->bhql', q, k_eff)
            attn = jnp.einsum('bhql,bkl->bhqk', q_lat, c_kv) / sqrt(hs)
            causal = jnp.tril(jnp.ones((T, T), dtype=bool))
            attn = jnp.where(causal[None, None], attn, -jnp.inf)
            attn = jax.nn.softmax(attn, axis=-1)
            y_lat = jnp.einsum('bhqk,bkl->bhql', attn, c_kv)
            y = jnp.einsum('bhql,hld->bqhd', y_lat, v_eff).reshape(B, T, C)
            return (y, c_kv)
        key = jax.random.key(seed)
        ks = jax.random.split(key, 7)
        B, T, C = (2, 256, 128)
        QL, KVL = (64, 64)
        return {'x': jax.random.normal(ks[0], (B, T, C), dtype=jnp.float32), 'W_dq': jax.random.normal(ks[1], (QL, C), dtype=jnp.float32) * W_SCALE, 'W_uq': jax.random.normal(ks[2], (C, QL), dtype=jnp.float32) * W_SCALE, 'W_dkv': jax.random.normal(ks[3], (KVL, C), dtype=jnp.float32) * W_SCALE, 'W_uk': jax.random.normal(ks[4], (C, KVL), dtype=jnp.float32) * W_SCALE, 'W_uv': jax.random.normal(ks[5], (C, KVL), dtype=jnp.float32) * W_SCALE, 'W_o': jax.random.normal(ks[6], (C, C), dtype=jnp.float32) * W_SCALE}
    _L0_attn_in = _L0_attn_setup()

    def _L0_ffn_setup():
        import jax, jax.numpy as jnp
        import numpy as np
        INT4_QMAX = 7.0

        def simulate_quantize_int4(w):
            scale = jnp.max(jnp.abs(w)) / INT4_QMAX
            q = jnp.clip(jnp.round(w / scale), -8.0, 7.0)
            return q * scale
        key = jax.random.key(seed)
        k_x, k_w, k_bias, k_a, k_b = jax.random.split(key, 5)
        d_in, features, rank = (128, 128, 16)
        x = jax.random.normal(k_x, (4, 1024, d_in), dtype=jnp.float32)
        kernel = jax.random.normal(k_w, (d_in, features), dtype=jnp.float32)
        bias = jax.random.normal(k_bias, (features,), dtype=jnp.float32)
        a = jax.random.normal(k_a, (d_in, rank), dtype=jnp.float32) * (1.0 / np.sqrt(d_in))
        b = jax.random.normal(k_b, (rank, features), dtype=jnp.float32) * 0.01
        return {'x': x, 'kernel': kernel, 'bias': bias, 'a': a, 'b': b}
    _L0_ffn_in = _L0_ffn_setup()

    def _L1_attn_setup():
        import jax, jax.numpy as jnp
        import numpy as np
        D_MODEL = 128
        NUM_HEADS = 16
        HEAD_DIM = D_MODEL // NUM_HEADS
        BATCH = 4
        SEQ = 256

        def circulant(x, c, b):
            d = c.shape[0]
            y = jnp.fft.irfft(jnp.fft.rfft(x, axis=-1) * jnp.fft.rfft(c), n=d, axis=-1)
            return y + b
        key = jax.random.key(seed)
        ks = jax.random.split(key, 9)
        scale = 1.0 / np.sqrt(D_MODEL)
        inp = {'x': jax.random.normal(ks[0], (BATCH, SEQ, D_MODEL), dtype=jnp.float32), 'wq_c': jax.random.normal(ks[1], (D_MODEL,), dtype=jnp.float32) * scale, 'wq_b': jnp.zeros((D_MODEL,), dtype=jnp.float32), 'wk_c': jax.random.normal(ks[2], (D_MODEL,), dtype=jnp.float32) * scale, 'wk_b': jnp.zeros((D_MODEL,), dtype=jnp.float32), 'wv_c': jax.random.normal(ks[3], (D_MODEL,), dtype=jnp.float32) * scale, 'wv_b': jnp.zeros((D_MODEL,), dtype=jnp.float32), 'wo_c': jax.random.normal(ks[4], (D_MODEL,), dtype=jnp.float32) * scale, 'wo_b': jnp.zeros((D_MODEL,), dtype=jnp.float32)}
        return inp
    _L1_attn_in = _L1_attn_setup()

    def _L1_ffn_setup():
        import jax, jax.numpy as jnp
        import numpy as np
        import math
        BETA = 0.9
        THRESHOLD = 1.0
        NUM_STEPS = 5
        ALPHA = 2.0

        @jax.custom_vjp
        def spike_fn(u):
            return (u > 0).astype(u.dtype)

        def _spike_fwd(u):
            return (spike_fn(u), u)

        def _spike_bwd(u, g):
            s = jnp.pi / 2.0 * ALPHA * u
            return (g * (ALPHA / 2.0) / (1.0 + s * s),)
        spike_fn.defvjp(_spike_fwd, _spike_bwd)
        key = jax.random.key(seed)
        k1, k2, k3 = jax.random.split(key, 3)
        n_embd = 128
        x = jax.random.normal(k1, (4, 256, n_embd), dtype=jnp.float32)
        W_fc = jax.random.normal(k2, (4 * n_embd, n_embd), dtype=jnp.float32) / math.sqrt(n_embd)
        W_proj = jax.random.normal(k3, (n_embd, 4 * n_embd), dtype=jnp.float32) / math.sqrt(4 * n_embd)
        return {'x': x, 'W_fc': W_fc, 'W_proj': W_proj}
    _L1_ffn_in = _L1_ffn_setup()
    _d = {'L0_attn_x': _L0_attn_in['x'], 'L0_attn_W_dq': _L0_attn_in['W_dq'], 'L0_attn_W_uq': _L0_attn_in['W_uq'], 'L0_attn_W_dkv': _L0_attn_in['W_dkv'], 'L0_attn_W_uk': _L0_attn_in['W_uk'], 'L0_attn_W_uv': _L0_attn_in['W_uv'], 'L0_attn_W_o': _L0_attn_in['W_o'], 'L0_ffn_kernel': _L0_ffn_in['kernel'], 'L0_ffn_bias': _L0_ffn_in['bias'], 'L0_ffn_a': _L0_ffn_in['a'], 'L0_ffn_b': _L0_ffn_in['b'], 'L1_attn_wq_c': _L1_attn_in['wq_c'], 'L1_attn_wq_b': _L1_attn_in['wq_b'], 'L1_attn_wk_c': _L1_attn_in['wk_c'], 'L1_attn_wk_b': _L1_attn_in['wk_b'], 'L1_attn_wv_c': _L1_attn_in['wv_c'], 'L1_attn_wv_b': _L1_attn_in['wv_b'], 'L1_attn_wo_c': _L1_attn_in['wo_c'], 'L1_attn_wo_b': _L1_attn_in['wo_b'], 'L1_ffn_W_fc': _L1_ffn_in['W_fc'], 'L1_ffn_W_proj': _L1_ffn_in['W_proj']}
    _x0 = _d['L0_attn_x']
    _d['L0_attn_x'] = jax.random.normal(jax.random.fold_in(jax.random.key(seed), 1), (4, 512, 128), dtype=_x0.dtype)
    del _x0
    return _d

def reference(L0_attn_x, L0_attn_W_dq, L0_attn_W_uq, L0_attn_W_dkv, L0_attn_W_uk, L0_attn_W_uv, L0_attn_W_o, L0_ffn_kernel, L0_ffn_bias, L0_ffn_a, L0_ffn_b, L1_attn_wq_c, L1_attn_wq_b, L1_attn_wk_c, L1_attn_wk_b, L1_attn_wv_c, L1_attn_wv_b, L1_attn_wo_c, L1_attn_wo_b, L1_ffn_W_fc, L1_ffn_W_proj):

    def _L0_attn_ref(x, W_dq, W_uq, W_dkv, W_uk, W_uv, W_o):
        import jax, jax.numpy as jnp
        import numpy as np
        from math import sqrt
        N_HEAD = 16
        W_SCALE = 0.02

        def _reference_tuple_inner(x, W_dq, W_uq, W_dkv, W_uk, W_uv, W_o):
            B, T, C = x.shape
            nh = N_HEAD
            hs = C // nh
            n_kvl = W_dkv.shape[0]
            k_eff = (W_dq.T @ W_uq.T @ W_uk).reshape(nh, hs, n_kvl)
            v_eff = jnp.transpose((W_uv.T @ W_o.T).reshape(n_kvl, nh, hs), (1, 0, 2))
            c_kv = x @ W_dkv.T
            q = x @ W_dq.T @ W_uq.T
            q = q.reshape(B, T, nh, hs)
            q_lat = jnp.einsum('bqhd,hdl->bhql', q, k_eff)
            attn = jnp.einsum('bhql,bkl->bhqk', q_lat, c_kv) / sqrt(hs)
            causal = jnp.tril(jnp.ones((T, T), dtype=bool))
            attn = jnp.where(causal[None, None], attn, -jnp.inf)
            attn = jax.nn.softmax(attn, axis=-1)
            y_lat = jnp.einsum('bhqk,bkl->bhql', attn, c_kv)
            y = jnp.einsum('bhql,hld->bqhd', y_lat, v_eff).reshape(B, T, C)
            return (y, c_kv)
        return _reference_tuple_inner(x, W_dq, W_uq, W_dkv, W_uk, W_uv, W_o)[0]

    def _L0_ffn_ref(x, kernel, bias, a, b):
        import jax, jax.numpy as jnp
        import numpy as np
        INT4_QMAX = 7.0

        def simulate_quantize_int4(w):
            scale = jnp.max(jnp.abs(w)) / INT4_QMAX
            q = jnp.clip(jnp.round(w / scale), -8.0, 7.0)
            return q * scale
        w = simulate_quantize_int4(kernel)
        y = jnp.einsum('bsd,df->bsf', x, w) + bias
        lora = jnp.einsum('bsr,rf->bsf', jnp.einsum('bsd,dr->bsr', x, a), b)
        return y + lora

    def _L1_attn_ref(x, wq_c, wq_b, wk_c, wk_b, wv_c, wv_b, wo_c, wo_b):
        import jax, jax.numpy as jnp
        import numpy as np
        D_MODEL = 128
        NUM_HEADS = 16
        HEAD_DIM = D_MODEL // NUM_HEADS
        BATCH = 4
        SEQ = 256

        def circulant(x, c, b):
            d = c.shape[0]
            y = jnp.fft.irfft(jnp.fft.rfft(x, axis=-1) * jnp.fft.rfft(c), n=d, axis=-1)
            return y + b
        bs, seq_len, dm = x.shape
        Q = circulant(x, wq_c, wq_b)
        K = circulant(x, wk_c, wk_b)
        V = circulant(x, wv_c, wv_b)
        Q = Q.reshape(bs, seq_len, NUM_HEADS, HEAD_DIM)
        K = K.reshape(bs, seq_len, NUM_HEADS, HEAD_DIM)
        V = V.reshape(bs, seq_len, NUM_HEADS, HEAD_DIM)
        scale = HEAD_DIM ** (-0.5)
        attn_logits = jnp.einsum('bqhd,bkhd->bhqk', Q, K) * scale
        attn_weights = jax.nn.softmax(attn_logits, axis=-1)
        out_heads = jnp.einsum('bhqk,bkhd->bqhd', attn_weights, V)
        out_merge = out_heads.reshape(bs, seq_len, dm)
        out = circulant(out_merge, wo_c, wo_b)
        return out

    def _L1_ffn_ref(x, W_fc, W_proj):
        import jax, jax.numpy as jnp
        import numpy as np
        import math
        BETA = 0.9
        THRESHOLD = 1.0
        NUM_STEPS = 5
        ALPHA = 2.0

        @jax.custom_vjp
        def spike_fn(u):
            return (u > 0).astype(u.dtype)

        def _spike_fwd(u):
            return (spike_fn(u), u)

        def _spike_bwd(u, g):
            s = jnp.pi / 2.0 * ALPHA * u
            return (g * (ALPHA / 2.0) / (1.0 + s * s),)
        spike_fn.defvjp(_spike_fwd, _spike_bwd)
        h = jnp.square(jax.nn.relu(jnp.einsum('bsd,fd->bsf', x, W_fc)))
        y = jnp.einsum('bsf,df->bsd', h, W_proj)

        def step(mem, _):
            reset = jax.lax.stop_gradient(spike_fn(mem - THRESHOLD))
            mem_new = BETA * mem + y - reset * THRESHOLD
            spk = spike_fn(mem_new - THRESHOLD)
            return (mem_new, spk)
        mem0 = jnp.zeros_like(y)
        _, spks = jax.lax.scan(step, mem0, None, length=NUM_STEPS)
        return jnp.sum(spks, axis=0) / NUM_STEPS
    x = L0_attn_x
    x = x + _L0_attn_ref(_layernorm(x, axis=-1), L0_attn_W_dq, L0_attn_W_uq, L0_attn_W_dkv, L0_attn_W_uk, L0_attn_W_uv, L0_attn_W_o)
    x = x + _L0_ffn_ref(_layernorm(x, axis=-1), L0_ffn_kernel, L0_ffn_bias, L0_ffn_a, L0_ffn_b)
    x = x + _L1_attn_ref(_layernorm(x, axis=-1), L1_attn_wq_c, L1_attn_wq_b, L1_attn_wk_c, L1_attn_wk_b, L1_attn_wv_c, L1_attn_wv_b, L1_attn_wo_c, L1_attn_wo_b)
    x = x + _L1_ffn_ref(_layernorm(x, axis=-1), L1_ffn_W_fc, L1_ffn_W_proj)
    return x

_drawn_inputs = setup_inputs


def setup_inputs(seed=0):
    import zlib

    import numpy as np

    out = dict(_drawn_inputs(seed))
    spreads = {'L1_attn_wq_b': (0.0, 0.8),
     'L1_attn_wk_b': (0.0, 2.0),
     'L1_attn_wv_b': (0.0, 0.8),
     'L1_attn_wo_b': (0.0, 0.8)}
    factors = {'L0_attn_W_dq': 8.0,
     'L0_attn_W_uq': 8.0,
     'L0_attn_W_dkv': 8.0,
     'L0_attn_W_uk': 8.0,
     'L0_attn_W_uv': 8.0,
     'L0_attn_W_o': 8.0,
     'L0_ffn_a': 8.0,
     'L0_ffn_b': 8.0,
     'L1_attn_wq_c': 5.73,
     'L1_attn_wk_c': 4.288,
     'L1_attn_wv_c': 4.231,
     'L1_attn_wo_c': 3.733,
     'L1_ffn_W_fc': 2.941,
     'L1_ffn_W_proj': 2.729}
    for name, (base, spread) in spreads.items():
        noise = np.random.default_rng([zlib.crc32(name.encode()), seed]).standard_normal(out[name].shape)
        drawn = base * np.exp(spread * noise) if base else spread * noise
        out[name] = jnp.asarray(drawn.astype(out[name].dtype))
    for name, factor in factors.items():
        out[name] = (out[name] * factor).astype(out[name].dtype)
    return out
```

```python
from contextlib import ExitStack

import concourse.bass as bass
from concourse import mybir

F32 = mybir.dt.float32
BF16 = mybir.dt.bfloat16
ALU = mybir.AluOpType
ACT = mybir.ActivationFunctionType
AX_X = mybir.AxisListType.X

P = 128
BATCHES, TOKENS, DIM = 4, 512, 128
HEADS, HEAD_DIM = 16, 8
BLOCKS = TOKENS // P
GROUP = 4
GROUPS = HEADS // GROUP
PAIRS = HEADS // 2
LATENT, RANK = 64, 16
FEATURES = 512
CHUNKS = FEATURES // P
SCALE = float(HEAD_DIM) ** -0.5
LN_EPS = 1e-5
INT4_MAX = 7.0
ROUND = 1.5 * 2.0 ** 23
DECAY, THRESHOLD, STEPS = 0.9, 1.0, 5
MASKED = -1e30

Q_PARTS = (0, 0, 0, 1, 1, 2)
K_PARTS = (0, 1, 2, 0, 1, 0)
TERM_ROWS = 2 * HEAD_DIM
MAX_ROW = len(Q_PARTS) * TERM_ROWS
ROWS = MAX_ROW + 4

TURN_BATCHES = 2
TURNS = BATCHES // TURN_BATCHES
PHASES = ((0, 0), (0, 1), (1, 0), (1, 1))
PHASE_SLOTS = GROUPS * BLOCKS
SLOTS = len(PHASES) * PHASE_SLOTS
T_GROUPS = len(PHASES) * GROUPS
LEAD = 5

UNITS = {
    0: (((0, (0, 2, 1, 3)), (1, (0, 1)), (1, (2, 3))), ((2, (0,)), (2, (1,)), (2, (2,))),
        ((2, (3,)), (3, (0,)), (3, (1,))), ((3, (2,)), (3, (3,)))),
    1: tuple(tuple((qb, (j,)) for j in range(GROUP)) for qb in range(BLOCKS)),
}
TILES = {
    0: (((0, 1), (2, 3)), ((0, 1), (2, 3)), ((0, 1, 2, 3),), ((0, 1, 2, 3),)),
    1: (((0, 1), (2, 3)),) * BLOCKS,
}


def layer_of(slot):
    return PHASES[slot // PHASE_SLOTS % len(PHASES)][0]


def units_of(slot):
    return UNITS[layer_of(slot)][slot % BLOCKS]


def tiles_of(slot):
    return TILES[layer_of(slot)][slot % BLOCKS]


UNITS_BEFORE = [0]
TILES_BEFORE = [0]
for _s in range(SLOTS + LEAD):
    UNITS_BEFORE.append(UNITS_BEFORE[-1] + len(units_of(_s)))
    TILES_BEFORE.append(TILES_BEFORE[-1] + len(tiles_of(_s)))
T_UNITS, T_TILES = UNITS_BEFORE[SLOTS], TILES_BEFORE[SLOTS]
MAX_READY = {g: UNITS_BEFORE[BLOCKS * (g + 1)] for g in range(T_GROUPS + 1)}
P_RING = 2

Q_CHAIN = ("norm", "turn", "q", "k", "v")
M_CHAIN = ("add", "norm", "turn", "linear", "turn2", "q", "k", "v")
E_CHAIN = ("turn", "out", "turn2", "fc0", "fc1", "fc2", "fc3", "proj", "spike2", "spike3", "spike4",
           "spike5", "count")
USES_MISC = {"q": ("turn", "q", "k", "v"), "m": ("turn", "linear", "turn2", "q", "k", "v"),
             "e": ("turn", "out", "turn2", "fc0", "fc1", "fc2", "fc3", "proj", "count")}


def place(chain, names, n, first, every=1):
    return {first + every * k: (chain, name, n) for k, name in enumerate(names)}


def side_steps():
    at = {s: [] for s in range(SLOTS)}
    for steps in (place("q", Q_CHAIN, 1, 0, 2), place("m", M_CHAIN, 0, 19), place("m", M_CHAIN, 1, 35),
                  place("e", E_CHAIN, 0, 51), place("q", Q_CHAIN, 2, 50, 2)):
        for s, step in steps.items():
            at[s].append(step)
    return at


SIDE_STEPS = side_steps()
TAIL = [("e", name, 1) for name in E_CHAIN]


def slot_misc(slot):
    group, at = divmod(slot, BLOCKS)
    uses = []
    if at == 3 and group + 1 < T_GROUPS:
        uses.append(("max", group + 1))
    if at == 2 and group > 0:
        uses.append(("heads", group - 1))
    return uses + [(c + "." + s, n) for c, s, n in SIDE_STEPS[slot] if s in USES_MISC[c]]


def tail_misc():
    uses = [("heads", T_GROUPS - 1)]
    for k, (c, s, n) in enumerate(TAIL):
        if s in USES_MISC[c]:
            uses.append((c + "." + s, n))
        if k == LEAD:
            uses.append(("max", T_GROUPS))
    return uses


SETUP = ("weights_turned", "weights_1", "weights_2", "weights_3", "circulants", "bias_columns",
         "fc_turned", "proj_turned")
FIRST = [(s, 0) for s in SETUP[:4]] + [("q." + s, 0) for s in USES_MISC["q"]] \
    + [(s, 0) for s in SETUP[4:]] + [("max", 0)]
MISC_ORDER = [u for s in range(SLOTS) for u in slot_misc(s)] + tail_misc()
FIRST_AT = {u: k for k, u in enumerate(FIRST)}
MISC_AT = {u: len(FIRST) + k for k, u in enumerate(MISC_ORDER)}
T_MISC = len(MISC_ORDER)

STACK_DMAS = len(Q_PARTS) + 2 * len(K_PARTS) + 1
STACK_DONE = 16 * STACK_DMAS


def build_program(nc, x_in, w_dq, w_uq, w_dkv, w_uk, w_uv, w_o, ffn_w, ffn_bias, ffn_a, ffn_b,
                  wq_c, wq_b, wk_c, wk_b, wv_c, wv_b, wo_c, wo_b, w_fc, w_proj, out):
    with ExitStack() as ctx:
        def sb(name, shape, dt=F32):
            return ctx.enter_context(nc.sbuf_tensor(name, shape, dt))

        def sem(name):
            return ctx.enter_context(nc.semaphore(name))

        score_tiles = [ctx.enter_context(nc.psum_tensor(f"score_tile{k}", [P, 2, 512], F32)) for k in range(2)]
        max_banks = [ctx.enter_context(nc.psum_tensor(f"max_bank{k}", [P, 512], F32)) for k in range(2)]
        heads_bank = ctx.enter_context(nc.psum_tensor("heads_bank", [P, TOKENS], F32))
        misc = ctx.enter_context(nc.psum_tensor("misc", [P, 512], F32))

        ident = sb("ident", [P, P])
        ident_bf = sb("ident_bf", [P, P], BF16)
        flip = sb("flip", [P, P])
        mask_qk = sb("mask_qk", [P, P], BF16)
        mask_kq = sb("mask_kq", [P, P], BF16)
        minus_ones = sb("minus_ones", [2, TOKENS], BF16)
        zero_rows = sb("zero_rows", [4, TOKENS], BF16)
        minus_half = sb("minus_half", [P, BLOCKS])
        one = sb("one", [1, 1])

        raw_dq, raw_dkv = sb("raw_dq", [LATENT, P]), sb("raw_dkv", [LATENT, P])
        raw_uq, raw_uk, raw_uv = sb("raw_uq", [P, LATENT]), sb("raw_uk", [P, LATENT]), sb("raw_uv", [P, LATENT])
        raw_o, raw_int4 = sb("raw_o", [P, P]), sb("raw_int4", [P, P])
        raw_a, raw_b = sb("raw_a", [P, RANK]), sb("raw_b", [RANK, P])
        raw_fc, raw_proj = sb("raw_fc", [P, CHUNKS, P]), sb("raw_proj", [P, FEATURES])
        hankel = sb("hankel", [P, 4, P])
        bias_rows = sb("bias_rows", [1, 2, P])
        bias_ordered = sb("bias_ordered", [1, 2, P])
        uq_t, o_t, a_t = sb("uq_t", [LATENT, P]), sb("o_t", [P, P]), sb("a_t", [RANK, P])
        qk_t, v_eff, k_eff_t = sb("qk_t", [P, P]), sb("v_eff", [LATENT, P]), sb("k_eff_t", [LATENT, P])
        wq = [sb(f"wq{l}", [P, P]) for l in range(2)]
        wk = [sb(f"wk{l}", [P, P]) for l in range(2)]
        wv = [sb(f"wv{l}", [P, P]) for l in range(2)]
        w_linear, w_out = sb("w_linear", [P, P]), sb("w_out", [P, P])
        fc_t, proj_t = sb("fc_t", [P, FEATURES]), sb("proj_t", [P, CHUNKS, P])
        bias_q, bias_k = sb("bias_q", [P, 1]), sb("bias_k", [P, 1])
        linear_bias, v_bias, out_bias = (sb(n, [P, P]) for n in ("linear_bias", "v_bias", "out_bias"))
        absmax, scale4, inv4 = sb("absmax", [P, 1]), sb("scale4", [P, 2]), sb("inv4", [P, 1])
        int4 = sb("int4", [P, P])

        q_stack = [sb(f"q_stack{n}", [P, PAIRS, TOKENS], BF16) for n in range(TURN_BATCHES)]
        k_stack = [sb(f"k_stack{n}", [P, PAIRS, 2, TOKENS], BF16) for n in range(TURN_BATCHES)]
        v_ones = [sb(f"v_ones{n}", [P, BLOCKS, HEADS, HEAD_DIM + 1]) for n in range(TURN_BATCHES)]
        heads = [sb(f"heads{n}", [P, BLOCKS, P]) for n in range(TURN_BATCHES)]
        probs = [sb(f"probs{k}", [P, GROUP * TOKENS]) for k in range(P_RING)]
        row_max = [sb(f"row_max{k}", [P, 2 * 2 * BLOCKS]) for k in range(2)]
        max_parts = [sb(f"max_parts{k}", [P, 2, 2 * 2 * BLOCKS], BF16) for k in range(2)]
        max_rows = [sb(f"max_rows{k}", [32, P], BF16) for k in range(2)]
        heads_t = [sb(f"heads_t{k}", [P, TOKENS]) for k in range(2)]
        inv_sum = sb("inv_sum", [P, BLOCKS, GROUP])

        x0 = [sb(f"x0_{n}", [P, BLOCKS, P]) for n in range(2)]
        x1, x1_biased, x2, x3 = (sb(n, [P, BLOCKS, P]) for n in ("x1", "x1_biased", "x2", "x3"))
        x2_biased = [sb(f"x2_biased{n}", [P, BLOCKS, P]) for n in range(2)]
        NORMS = ("q", "m", "m2", "e")
        stats = {k: sb("stats_" + k, [P, BLOCKS, 6]) for k in NORMS}
        mean_var = {k: sb("mean_var_" + k, [P, BLOCKS, 2]) for k in NORMS}
        var_eps = {k: sb("var_eps_" + k, [P, BLOCKS]) for k in NORMS}
        rstd = {k: sb("rstd_" + k, [P, BLOCKS]) for k in NORMS}
        normed = {k: sb("normed_" + k, [P, BLOCKS, P]) for k in NORMS}
        normed_t = {k: sb("normed_t_" + k, [P, TOKENS]) for k in NORMS}
        full = {t: sb(f"full_{t}", [P, TOKENS]) for t in "qk"}
        rest = sb("rest", [P, TOKENS])
        parts = {t: sb(f"parts_{t}", [P, 3, TOKENS], BF16) for t in "qk"}
        heads_all_t = sb("heads_all_t", [P, TOKENS])
        relu = sb("relu", [P, TOKENS])
        hidden = sb("hidden", [P, CHUNKS, TOKENS])
        drive, decayed, membrane = sb("drive", [P, TOKENS]), sb("decayed", [P, TOKENS]), sb("membrane", [P, TOKENS])
        spikes = sb("spikes", [P, STEPS, TOKENS], BF16)
        result = [sb(f"result{n}", [P, BLOCKS, P]) for n in range(2)]

        x_loaded = [sem(f"x_loaded{n}") for n in range(2)]
        w_loaded, w1_loaded, doubled = sem("w_loaded"), sem("w1_loaded"), sem("doubled")
        consts_ready, pool_step = sem("consts_ready"), sem("pool_step")
        stacks_zeroed, minus_loaded, v_prepared = sem("stacks_zeroed"), sem("minus_loaded"), sem("v_prepared")
        absmax_ready, absmax_all, int4_step = sem("absmax_ready"), sem("absmax_all"), sem("int4_step")
        int4_ready, bias_ready = sem("int4_ready"), sem("bias_ready")
        misc_full, misc_free = sem("misc_full"), sem("misc_free")
        unit_full, unit_read = sem("unit_full"), sem("unit_read")
        max_high, max_split = sem("max_high"), sem("max_split")
        max_loaded = [sem(f"max_loaded{k}") for k in range(2)]
        tile_full, tile_read = sem("tile_full"), sem("tile_read")
        pv_done, heads_free = sem("pv_done"), sem("heads_free")
        inverted = sem("inverted")
        stack_loaded = [sem(f"stack_loaded{n}") for n in range(TURN_BATCHES)]
        stats_done = {k: sem("stats_done_" + k) for k in NORMS}
        mean_ready = {k: sem("mean_ready_" + k) for k in NORMS}
        eps_added = {k: sem("eps_added_" + k) for k in NORMS}
        rstd_ready = {k: sem("rstd_ready_" + k) for k in NORMS}
        normed_ready = {k: sem("normed_ready_" + k) for k in NORMS}
        rest_ready = {(l, t): sem(f"rest_ready_{t}{l}") for l in range(2) for t in "qk"}
        middle_ready = {(l, t): sem(f"middle_ready_{t}{l}") for l in range(2) for t in "qk"}
        low_ready = {(l, t): sem(f"low_ready_{t}{l}") for l in range(2) for t in "qk"}
        x1_ready, x1_biased_ready, x2_biased_ready = sem("x1_ready"), sem("x1_biased_ready"), sem("x2_biased_ready")
        relu_ready, spike_ready, decay_ready = sem("relu_ready"), sem("spike_ready"), sem("decay_ready")
        membrane_ready, result_ready = sem("membrane_ready"), sem("result_ready")
        stored = [sem(f"stored{n}") for n in range(2)]
        waited = sem("waited")

        circ = nc.dram_tensor("circ_twice", (4, 2 * P), F32, kind="Internal")
        circ_ap = circ.ap()

        def misc_at(use, turn):
            return turn * T_MISC + MISC_AT[use] if turn is not None else FIRST_AT[use]

        def run_of(chain, n, turn):
            return 0 if turn is None else turn * TURN_BATCHES + n

        def wait(eng, semaphore, value):
            if not isinstance(value, int) or value > 0:
                eng.wait_ge(semaphore, value)

        def wait_apart(eng, semaphore, value):
            eng.wait_ge(semaphore, value)
            eng.sem_inc(waited, 1)

        def q_blocks(l, kb):
            first = kb * P if l == 0 else 0
            return first, TOKENS - first

        def prob_view(k, l, kb, j):
            width = q_blocks(l, kb)[1]
            return probs[k][:, j * width:(j + 1) * width]

        def for_pairs(tile, rows):
            return tile[:].rearrange("p (o q) -> p o q", o=1).to_broadcast([rows, PAIRS, TOKENS])

        block = ctx.enter_context(nc.Block())

        @block.sync
        def _(sp):
            def load_x(n, batch):
                sp.dma_start(x0[n][:], x_in[batch].rearrange("(b p) c -> p b c", p=P)).then_inc(x_loaded[n], 16)

            load_x(0, 0)
            for dst, src in ((raw_uq, w_uq), (raw_o, w_o), (raw_a, ffn_a), (raw_dq, w_dq), (raw_uv, w_uv),
                             (raw_b, ffn_b), (raw_int4, ffn_w), (raw_dkv, w_dkv), (raw_uk, w_uk)):
                sp.dma_start(dst[:], src).then_inc(w_loaded, 16)
            for w, c in enumerate((wq_c, wk_c, wv_c, wo_c)):
                twice = circ_ap[w:w + 1, :].rearrange("o (r n) -> o r n", r=2)
                for r in range(2):
                    sp.dma_start(twice[:, r, :], c.rearrange("(o n) -> o n", o=1)).then_inc(doubled, 16)
            sp.wait_ge(stacks_zeroed, 3)
            for n in range(TURN_BATCHES):
                for half in range(2):
                    rows = k_stack[n][MAX_ROW + half:ROWS:2, :, half, :]
                    sp.dma_start(rows, for_pairs(minus_ones, 2)).then_inc(minus_loaded, 16)
            for n in range(2):
                sp.sem_inc(stored[n], 16)

            def load_parts(l, n, t, part, high_at, run):
                if part == 0:
                    sp.wait_ge(misc_free, high_at + 1)
                else:
                    sp.wait_ge((middle_ready, low_ready)[part - 1][(l, t)], run + 1)
                for term, own in enumerate(Q_PARTS if t == "q" else K_PARTS):
                    if own != part:
                        continue
                    first = term * TERM_ROWS
                    if t == "q":
                        sp.dma_start(q_stack[n][first:first + TERM_ROWS, :, :],
                                     parts[t][:, part, :]).then_inc(stack_loaded[n], 16)
                    else:
                        for half in range(2):
                            sp.dma_start(k_stack[n][first + half:first + TERM_ROWS:2, :, half, :],
                                         parts[t][64 * half:64 * half + 64, part, :]
                                         ).then_inc(stack_loaded[n], 16)

            def side(chain, step, n, turn):
                if chain in ("q", "m") and step in ("q", "k"):
                    l = 0 if chain == "q" else 1
                    high_at = misc_at((chain + "." + step, n), turn)
                    run = run_of(chain, n, turn)
                    if step == "q":
                        sp.wait_ge(misc_free, high_at + 1)
                        sp.dma_start(q_stack[n % 2][MAX_ROW:ROWS, :, :],
                                     for_pairs(zero_rows, 4)
                                     ).then_inc(stack_loaded[n % 2], 16)
                    for part in range(3):
                        load_parts(l, n % 2, step, part, high_at, run)
                if (chain, step, n) == ("m", "norm", 0):
                    sp.wait_ge(x1_ready, run_of("m", 0, turn) + 1)
                    load_x(0, BATCHES - 2)
                if (chain, step, n) == ("m", "norm", 1):
                    sp.wait_ge(x1_ready, run_of("m", 1, turn) + 1)
                    load_x(1, BATCHES - 1)
                if (chain, step) == ("e", "count"):
                    sp.wait_ge(result_ready, run_of("e", n, turn) + 1)
                    dst = out[turn * TURN_BATCHES + n].rearrange("(b p) c -> p b c", p=P)
                    sp.dma_start(dst, result[n][:]).then_inc(stored[n], 16)

            def load_max_rows(group, use):
                l, n = PHASES[group // GROUPS % len(PHASES)]
                g = group % GROUPS
                sp.wait_ge(misc_free, use + 1)
                sp.dma_start(q_stack[n][MAX_ROW:ROWS, 2 * g:2 * g + 2, :].rearrange("p r (b q) -> p (r b) q", b=BLOCKS),
                             max_rows[group % 2][:]).then_inc(max_loaded[group % 2], 16)

            for step in ("q", "k"):
                side("q", step, 0, None)
            load_x(1, 1)
            sp.wait_ge(doubled, 16 * 8)
            for w in range(4):
                window = bass.AP(tensor=circ_ap.tensor, offset=w * 2 * P, ap=[[1, P], [1, P]])
                sp.dma_start(hankel[:, w, :], window).then_inc(w1_loaded, 16)
            for k, b in enumerate((wq_b, wk_b)):
                sp.dma_start(bias_rows[:, k, :], b.rearrange("(o n) -> o n", o=1)).then_inc(w1_loaded, 16)
            for dst, src in ((linear_bias, ffn_bias), (v_bias, wv_b), (out_bias, wo_b)):
                sp.dma_start(dst[:], src.rearrange("(o n) -> o n", o=1).to_broadcast([P, P])).then_inc(w1_loaded, 16)
            sp.dma_start(raw_fc[:], w_fc.rearrange("(f p) c -> p f c", p=P)).then_inc(w1_loaded, 16)
            sp.dma_start(raw_proj[:], w_proj).then_inc(w1_loaded, 16)
            load_max_rows(0, FIRST_AT[("max", 0)])
            with sp.Fori(0, TURNS) as turn:
                for s in range(SLOTS):
                    for use in slot_misc(s):
                        if use[0] == "max":
                            load_max_rows(use[1], misc_at(use, turn))
                    for step in SIDE_STEPS[s]:
                        side(*step, turn)
                for k, step in enumerate(TAIL):
                    side(*step, turn)
                    if k == LEAD:
                        load_max_rows(T_GROUPS, misc_at(("max", T_GROUPS), turn))
            for n in range(2):
                sp.wait_ge(stored[n], 16 + 16 * TURNS)
            sp.wait_ge(max_loaded[0], 16 * (T_GROUPS // 2 * TURNS + 1))
            sp.wait_ge(stack_loaded[0], STACK_DONE * (2 * TURNS + 1))
            sp.wait_ge(x_loaded[0], 16 * (TURNS + 1))
            sp.wait_ge(x_loaded[1], 16 * (TURNS + 1))

        @block.gpsimd
        def _(pool):
            steps = [0]

            def then_wait(ins):
                steps[0] += 1
                ins.then_inc(pool_step, 1)
                pool.wait_ge(pool_step, steps[0])

            pool.memset(ident[:], 0.0).then_inc(pool_step, 1)
            pool.memset(flip[:], 0.0).then_inc(pool_step, 1)
            pool.memset(mask_qk[:], 0.0).then_inc(pool_step, 1)
            pool.memset(mask_kq[:], 0.0).then_inc(pool_step, 1)
            pool.memset(minus_half[:], -0.5).then_inc(pool_step, 1)
            pool.memset(one[:], 1.0).then_inc(pool_step, 1)
            steps[0] = 6
            pool.wait_ge(pool_step, steps[0])
            then_wait(pool.affine_select(out=ident[:], in_=ident[:], pattern=[[-1, P]], compare_op=ALU.not_equal,
                                         fill=1.0, base=0, channel_multiplier=1))
            then_wait(pool.tensor_copy(ident_bf[:], ident[:]))
            then_wait(pool.affine_select(out=flip[:], in_=flip[:], pattern=[[1, P]], compare_op=ALU.not_equal,
                                         fill=1.0, base=-P, channel_multiplier=1))
            then_wait(pool.affine_select(out=flip[:], in_=flip[:], pattern=[[1, P]], compare_op=ALU.not_equal,
                                         fill=1.0, base=0, channel_multiplier=1))
            pool.affine_select(out=mask_qk[:], in_=mask_qk[:], pattern=[[-1, P]], compare_op=ALU.is_ge,
                               fill=MASKED, base=0, channel_multiplier=1).then_inc(consts_ready, 1)
            pool.affine_select(out=mask_kq[:], in_=mask_kq[:], pattern=[[1, P]], compare_op=ALU.is_ge,
                               fill=MASKED, base=0, channel_multiplier=-1).then_inc(consts_ready, 1)
            pool.wait_ge(absmax_ready, 1)
            pool.partition_all_reduce(scale4[:, 0:1], absmax[:], P, bass.bass_isa.ReduceOp.max).then_inc(absmax_all, 1)

            def inverse_std(k, run):
                wait_apart(pool, mean_ready[k], run + 1)
                pool.tensor_scalar(var_eps[k][:], mean_var[k][:, :, 1], 1.0, LN_EPS, ALU.mult, ALU.add
                                   ).then_inc(eps_added[k], 1)
                pool.wait_ge(eps_added[k], run + 1)
                pool.tensor_tensor(rstd[k][:], var_eps[k][:], minus_half[:], ALU.pow).then_inc(rstd_ready[k], 1)

            def split(l, t, use, run):
                key = (l, t)
                pool.wait_ge(misc_free, use + 1)
                pool.tensor_tensor(rest[:], full[t][:], parts[t][:, 0, :], ALU.subtract
                                   ).then_inc(rest_ready[key], 1)
                wait_apart(pool, rest_ready[key], run + 1)
                pool.tensor_scalar(parts[t][:, 1, :], rest[:], 1.0, 0.0, ALU.mult, ALU.add
                                   ).then_inc(middle_ready[key], 1)
                pool.wait_ge(middle_ready[key], run + 1)
                pool.tensor_tensor(parts[t][:, 2, :], rest[:], parts[t][:, 1, :], ALU.subtract
                                   ).then_inc(low_ready[key], 1)
                pool.wait_ge(low_ready[key], run + 1)

            def rows_of(tile):
                return tile[:].rearrange("p (o c) -> p o c", o=1).to_broadcast([P, BLOCKS, P])

            def side(chain, step, n, turn):
                run = run_of(chain, n, turn)
                if chain in ("q", "m") and step in ("q", "k"):
                    split(0 if chain == "q" else 1, step, misc_at((chain + "." + step, n), turn), run)
                elif (chain, step) in (("q", "norm"), ("m", "norm")):
                    inverse_std(chain, run)
                elif (chain, step) == ("m", "add"):
                    pool.wait_ge(misc_free, misc_at(("heads", GROUPS * (n + 1) - 1), turn) + 1)
                    pool.tensor_tensor(x1[:], x0[n][:], heads[n][:], ALU.add).then_inc(x1_ready, 1)
                    pool.wait_ge(x1_ready, run + 1)
                    pool.tensor_tensor(x1_biased[:], x1[:], rows_of(linear_bias), ALU.add).then_inc(x1_biased_ready, 1)
                elif (chain, step) == ("m", "linear"):
                    inverse_std("m2", run)
                    pool.tensor_tensor(x2_biased[n][:], x2[:], rows_of(out_bias), ALU.add).then_inc(x2_biased_ready, 1)
                elif (chain, step) == ("e", "out"):
                    inverse_std("e", run)

            for step in Q_CHAIN:
                side("q", step, 0, None)
            pool.wait_ge(w1_loaded, 16 * 11)
            for k, (a, b, order) in enumerate(((HEAD_DIM, 2, "o (r a d) -> o d a r"), (2, HEAD_DIM, "o (r a d) -> o a d r"))):
                pool.tensor_copy(bias_ordered[:, k, :].rearrange("o (x y r) -> o x y r", x=a, y=b),
                                 bias_rows[:, k, :].rearrange(order, a=2, d=HEAD_DIM)).then_inc(bias_ready, 1)
            with pool.Fori(0, TURNS) as turn:
                for s in range(SLOTS):
                    for step in SIDE_STEPS[s]:
                        side(*step, turn)
                for step in TAIL:
                    side(*step, turn)

        @block.tensor
        def _(pe):
            def open_misc(use):
                wait(pe, misc_free, use)

            def turn_blocks(src):
                for b in range(BLOCKS):
                    last = pe.transpose(misc[:, b * P:(b + 1) * P], src[:, b, :], ident[:])
                last.then_inc(misc_full, 1)

            def by_token(src_t, w):
                for b in range(BLOCKS):
                    last = pe.matmul(misc[:, b * P:(b + 1) * P], src_t[:, b * P:(b + 1) * P], w[:], start=True, stop=True)
                last.then_inc(misc_full, 1)

            def side(chain, step, n, turn):
                if step not in USES_MISC[chain]:
                    return
                run = run_of(chain, n, turn)
                l = 0 if chain == "q" else 1
                k2 = {"q": "q", "m": "m2"}.get(chain)
                open_misc(misc_at((chain + "." + step, n), turn))
                if step == "turn" and chain != "e":
                    pe.wait_ge(normed_ready[chain], run + 1)
                    turn_blocks(normed[chain])
                elif step == "turn":
                    turn_blocks(heads[n])
                elif step == "turn2":
                    k = "m2" if chain == "m" else "e"
                    pe.wait_ge(normed_ready[k], run + 1)
                    turn_blocks(normed[k])
                elif step in ("q", "k"):
                    w = (wq if step == "q" else wk)[l]
                    pe.matmul(misc[:], w[:], normed_t[k2][:], start=True, stop=True).then_inc(misc_full, 1)
                elif step == "v":
                    by_token(normed_t[k2], wv[l])
                elif step == "linear":
                    by_token(normed_t["m"], w_linear)
                elif step == "out":
                    by_token(heads_all_t, w_out)
                elif step.startswith("fc"):
                    f = int(step[2:])
                    pe.matmul(misc[:], fc_t[:, f * P:(f + 1) * P], normed_t["e"][:], start=True, stop=True
                              ).then_inc(misc_full, 1)
                elif step == "proj":
                    for f in range(CHUNKS):
                        last = pe.matmul(misc[:], proj_t[:, f, :], hidden[:, f, :], start=(f == 0), stop=(f == CHUNKS - 1))
                    last.then_inc(misc_full, 1)
                elif step == "count":
                    pe.wait_ge(spike_ready, STEPS * run + STEPS)
                    for b in range(BLOCKS):
                        for k in range(STEPS):
                            last = pe.matmul(misc[:, b * P:(b + 1) * P], spikes[:, k, b * P:(b + 1) * P], ident_bf[:],
                                             start=(k == 0), stop=(k == STEPS - 1))
                    last.then_inc(misc_full, 1)

            def score_unit(slot, u, turn):
                l, n = PHASES[slot // PHASE_SLOTS % len(PHASES)]
                g = slot // BLOCKS % GROUPS
                qb, js = units_of(slot)[u]
                count = turn * T_UNITS + UNITS_BEFORE[slot] + u
                bank = max_banks[(UNITS_BEFORE[slot] + u) % 2]
                if slot % PHASE_SLOTS == 0 and u == 0:
                    pe.wait_ge(stack_loaded[n], turn * 2 * STACK_DONE + (l + 1) * STACK_DONE)
                wait(pe, unit_read, count - 1)
                width = (qb + 1) * P if l == 0 else TOKENS
                for k, j in enumerate(js):
                    pair, half = 2 * g + j // 2, j % 2
                    last = pe.matmul(bank[:, k * width:(k + 1) * width], q_stack[n][0:ROWS, pair, qb * P:(qb + 1) * P],
                                     k_stack[n][0:ROWS, pair, half, 0:width], start=True, stop=(l == 1))
                    if l == 0:
                        last = pe.matmul(bank[:, (k + 1) * width - P:(k + 1) * width], ident_bf[:], mask_qk[:],
                                         start=False, stop=True)
                last.then_inc(unit_full, 1)

            def turn_max(group, use, turn):
                open_misc(use)
                pe.wait_ge(max_split, turn * T_GROUPS + group + 1)
                pe.transpose(misc[0:32, 0:P // 2].bitcast(BF16), max_parts[group % 2][:].rearrange("p a c -> p (a c)"),
                             ident_bf[:]).then_inc(misc_full, 1)

            def turn_heads(group, use, turn):
                open_misc(use)
                pe.wait_ge(heads_free, turn * T_GROUPS + group + 2)
                for b in range(BLOCKS):
                    last = pe.transpose(misc[:, b * P:(b + 1) * P], heads_t[group % 2][:, b * P:(b + 1) * P], ident[:])
                last.then_inc(misc_full, 1)

            def score_tile(slot, t, turn):
                l, n = PHASES[slot // PHASE_SLOTS]
                group, kb = divmod(slot, BLOCKS)
                g = group % GROUPS
                index = TILES_BEFORE[slot] + t
                tile = score_tiles[index % 2]
                if kb == 0 and t == 0:
                    pe.wait_ge(max_loaded[group % 2], turn * (16 * T_GROUPS // 2) + 16 * (group // 2 + 1))
                pe.wait_ge(tile_read, turn * T_TILES + index + 1)
                js = tiles_of(slot)[t]
                first, width = q_blocks(l, kb)
                per_bank = min(len(js), 512 // width)
                for k, j in enumerate(js):
                    pair, half = 2 * g + j // 2, j % 2
                    at = tile[:, k // per_bank, (k % per_bank) * width:(k % per_bank + 1) * width]
                    last = pe.matmul(at, k_stack[n][0:ROWS, pair, half, kb * P:(kb + 1) * P],
                                     q_stack[n][0:ROWS, pair, first:TOKENS], start=True, stop=(l == 1))
                    if l == 0:
                        last = pe.matmul(at[:, 0:P], ident_bf[:], mask_kq[:], start=False, stop=True)
                last.then_inc(tile_full, 1)

            def times_v(slot, js, turn):
                l, n = PHASES[slot // PHASE_SLOTS]
                group, kb = divmod(slot, BLOCKS)
                first, width = q_blocks(l, kb)
                if js[0] == 0:
                    pe.wait_ge(tile_read, turn * T_TILES + TILES_BEFORE[slot + 1] + 2)
                    if kb == 0:
                        pe.wait_ge(heads_free, turn * T_GROUPS + group + 1)
                for j in js:
                    h = GROUP * (group % GROUPS) + j
                    last = pe.matmul(heads_bank[32 * j:32 * j + HEAD_DIM + 1, first:TOKENS], v_ones[n][:, kb, h, :],
                                     prob_view(slot % P_RING, l, kb, j), start=(kb == 0), stop=(kb == BLOCKS - 1),
                                     skip_group_check=True, tile_position=(0, 32 * j))
                if js[-1] == GROUP - 1:
                    last.then_inc(pv_done, 1)

            def setup(name):
                open_misc(FIRST_AT[(name, 0)])
                if name == "weights_turned":
                    pe.wait_ge(consts_ready, 2)
                    pe.wait_ge(w_loaded, 16 * 9)
                    pe.transpose(misc[0:LATENT, 0:P], raw_uq[:], ident[:])
                    pe.transpose(misc[:, P:2 * P], raw_o[:], ident[:])
                    last = pe.transpose(misc[0:RANK, 2 * P:3 * P], raw_a[:], ident[:])
                elif name == "weights_1":
                    pe.matmul(misc[:, 0:P], raw_dq[:], uq_t[:], start=True, stop=True)
                    pe.matmul(misc[:, P:2 * P], uq_t[:], raw_dq[:], start=True, stop=True)
                    pe.matmul(misc[0:LATENT, 2 * P:3 * P], raw_uv[:], o_t[:], start=True, stop=True)
                    last = pe.matmul(misc[:, 3 * P:4 * P], a_t[:], raw_b[:], start=True, stop=True)
                elif name == "weights_2":
                    pe.matmul(misc[0:LATENT, 0:P], raw_uk[:], qk_t[:], start=True, stop=True)
                    last = pe.matmul(misc[:, P:2 * P], raw_dkv[:], v_eff[:], start=True, stop=True)
                elif name == "weights_3":
                    last = pe.matmul(misc[:, 0:P], raw_dkv[:], k_eff_t[:], start=True, stop=True)
                elif name == "circulants":
                    pe.wait_ge(w1_loaded, 16 * 11)
                    for w in range(4):
                        last = pe.matmul(misc[:, w * P:(w + 1) * P], flip[:], hankel[:, w, :], start=True, stop=True)
                elif name == "bias_columns":
                    pe.wait_ge(bias_ready, 2)
                    for k in range(2):
                        last = pe.matmul(misc[:, k:k + 1], bias_ordered[:, k, :], one[:], start=True, stop=True)
                elif name == "fc_turned":
                    for f in range(CHUNKS):
                        last = pe.transpose(misc[:, f * P:(f + 1) * P], raw_fc[:, f, :], ident[:])
                elif name == "proj_turned":
                    for f in range(CHUNKS):
                        last = pe.transpose(misc[:, f * P:(f + 1) * P], raw_proj[:, f * P:(f + 1) * P], ident[:])
                last.then_inc(misc_full, 1)

            for name in SETUP[:4]:
                setup(name)
            for step in Q_CHAIN:
                side("q", step, 0, None)
            for name in SETUP[4:]:
                setup(name)
            pe.wait_ge(minus_loaded, 16 * 4)
            pe.wait_ge(v_prepared, 3)
            for s in range(LEAD):
                for u in range(len(units_of(s))):
                    score_unit(s, u, 0)
            turn_max(0, FIRST_AT[("max", 0)], 0)

            with pe.Fori(0, TURNS) as turn:
                for s in range(SLOTS):
                    todo = list(range(len(units_of(s + LEAD)))) if s + LEAD < SLOTS else []

                    def some_units(k):
                        for u in todo[:k]:
                            score_unit(s + LEAD, u, turn)
                        del todo[:k]

                    last_tile = len(tiles_of(s)) - 1
                    score_tile(s, 0, turn)
                    some_units(1)
                    if s > 0:
                        times_v(s - 1, (0, 1, 2, 3), turn)
                    some_units(1)
                    if last_tile:
                        score_tile(s, 1, turn)
                    some_units(len(todo))
                    for use in slot_misc(s):
                        if use[0] == "max":
                            turn_max(use[1], misc_at(use, turn), turn)
                        elif use[0] == "heads":
                            turn_heads(use[1], misc_at(use, turn), turn)
                    for step in SIDE_STEPS[s]:
                        side(*step, turn)
                times_v(SLOTS - 1, (0, 1, 2, 3), turn)
                turn_heads(T_GROUPS - 1, misc_at(("heads", T_GROUPS - 1), turn), turn)
                for k, step in enumerate(TAIL):
                    side(*step, turn)
                    if k < LEAD:
                        for u in range(len(units_of(k))):
                            score_unit(k, u, turn + 1)
                    if k == LEAD:
                        turn_max(T_GROUPS, misc_at(("max", T_GROUPS), turn), turn)

        @block.vector
        def _(dve):
            def max_view(group):
                return row_max[group % 2][:].rearrange("p (a r b) -> p a r b", a=2, r=2)

            def reduce_unit(slot, u, turn):
                l, group = layer_of(slot), slot // BLOCKS
                qb, js = units_of(slot)[u]
                count = turn * T_UNITS + UNITS_BEFORE[slot] + u
                bank = max_banks[(UNITS_BEFORE[slot] + u) % 2]
                width = (qb + 1) * P if l == 0 else TOKENS
                to = max_view(group)
                scores = bank[:, 0:len(js) * width]
                if len(js) == 4:
                    to, scores = to[:, :, :, qb], scores.rearrange("p (a r q) -> p a r q", a=2, r=2)
                elif len(js) == 2:
                    to, scores = to[:, :, js[0] // 2, qb], scores.rearrange("p (a q) -> p a q", a=2)
                else:
                    to = to[:, js[0] % 2, js[0] // 2, qb:qb + 1]
                dve.wait_ge(unit_full, count + 1)
                dve.tensor_reduce(to, scores, AX_X, ALU.max).then_inc(unit_read, 1)

            def split_max(group, turn):
                dve.wait_ge(unit_read, turn * T_UNITS + MAX_READY[group])
                dve.tensor_copy(max_parts[group % 2][:, 0, :], row_max[group % 2][:]).then_inc(max_high, 1)
                dve.wait_ge(max_high, turn * T_GROUPS + group + 1)
                dve.tensor_tensor(max_parts[group % 2][:, 1, :], row_max[group % 2][:], max_parts[group % 2][:, 0, :],
                                  ALU.subtract).then_inc(max_split, 1)

            def divide_heads(group, use, turn):
                l, n = PHASES[group // GROUPS]
                g = group % GROUPS
                view = misc[:].rearrange("p (b j c) -> p b j c", b=BLOCKS, j=GROUP)
                dve.wait_ge(misc_full, use + 1)
                dve.reciprocal(inv_sum[:], view[:, :, :, HEAD_DIM]).then_inc(inverted, 1)
                dve.wait_ge(inverted, turn * T_GROUPS + group + 1)
                to = heads[n][:, :, g * 32:(g + 1) * 32].rearrange("p b (j d) -> p b j d", j=GROUP)
                inv = inv_sum[:].rearrange("p b (j o) -> p b j o", o=1).to_broadcast([P, BLOCKS, GROUP, HEAD_DIM])
                dve.tensor_tensor(to, view[:, :, :, 0:HEAD_DIM], inv, ALU.mult).then_inc(misc_free, 1)

            def statistics(k, x, run):
                for b in range(BLOCKS):
                    last = dve.bn_stats(stats[k][:, b, :], x[:, b, :])
                last.then_inc(stats_done[k], 1)
                wait_apart(dve, stats_done[k], run + 1)
                for b in range(BLOCKS):
                    last = dve.bn_aggr(mean_var[k][:, b, :], stats[k][:, b, :])
                last.then_inc(mean_ready[k], 1)

            def normalise(k, x, run):
                dve.wait_ge(rstd_ready[k], run + 1)
                for b in range(BLOCKS):
                    last = dve.tensor_scalar(normed[k][:, b, :], x[:, b, :], mean_var[k][:, b, 0:1], rstd[k][:, b:b + 1],
                                             ALU.subtract, ALU.mult)
                last.then_inc(normed_ready[k], 1)

            misc_blocks = misc[:].rearrange("p (b c) -> p b c", b=BLOCKS)

            def side(chain, step, n, turn):
                run = run_of(chain, n, turn)
                if (chain, step) == ("q", "norm"):
                    if turn is None:
                        dve.wait_ge(x_loaded[0], 16)
                    else:
                        dve.wait_ge(x_loaded[n % 2], turn * 16 + 16 * (1 + n // 2))
                    statistics("q", x0[n % 2], run)
                elif (chain, step) == ("q", "turn"):
                    normalise("q", x0[n % 2], run)
                elif (chain, step) == ("m", "norm"):
                    dve.wait_ge(x1_ready, run + 1)
                    statistics("m", x1, run)
                elif (chain, step) == ("m", "turn"):
                    normalise("m", x1, run)
                elif (chain, step) == ("m", "linear"):
                    dve.wait_ge(misc_full, misc_at(("m.linear", n), turn) + 1)
                    dve.wait_ge(x1_biased_ready, run + 1)
                    dve.wait_ge(x2_biased_ready, run + 1)
                    dve.tensor_tensor(x2[:], misc_blocks, x1_biased[:], ALU.add).then_inc(misc_free, 1)
                    dve.wait_ge(misc_free, misc_at(("m.linear", n), turn) + 1)
                    statistics("m2", x2, run)
                elif (chain, step) == ("m", "turn2"):
                    normalise("m2", x2, run)
                elif (chain, step) == ("m", "v"):
                    dve.wait_ge(misc_full, misc_at(("m.v", n), turn) + 1)
                    to = v_ones[n][:].rearrange("p b h c -> p (b h) c")[:, :, 0:HEAD_DIM]
                    dve.tensor_tensor(to, misc[:].rearrange("p (m d) -> p m d", d=HEAD_DIM),
                                      v_bias[:].rearrange("p (o c) -> p o c", o=1).to_broadcast([P, BLOCKS, P]),
                                      ALU.add).then_inc(misc_free, 1)
                elif (chain, step) == ("e", "out"):
                    dve.wait_ge(misc_full, misc_at(("e.out", n), turn) + 1)
                    dve.wait_ge(x2_biased_ready, run + 2)
                    dve.tensor_tensor(x3[:], misc_blocks, x2_biased[n][:], ALU.add).then_inc(misc_free, 1)
                    dve.wait_ge(misc_free, misc_at(("e.out", n), turn) + 1)
                    statistics("e", x3, run)
                elif (chain, step) == ("e", "turn2"):
                    normalise("e", x3, run)
                elif chain == "e" and step.startswith("spike"):
                    k = int(step[5:])
                    first = run * (STEPS - 1) + k - 2
                    mem = drive if k == 2 else membrane
                    if k == 2:
                        dve.wait_ge(misc_free, misc_at(("e.proj", n), turn) + 1)
                        dve.tensor_scalar(spikes[:, 0, :], drive[:], THRESHOLD, None, ALU.is_gt).then_inc(spike_ready, 1)
                    dve.scalar_tensor_tensor(out=decayed[:], in0=mem[:], scalar=DECAY, in1=drive[:],
                                             op0=ALU.mult, op1=ALU.add).then_inc(decay_ready, 1)
                    dve.wait_ge(decay_ready, first + 1)
                    dve.wait_ge(spike_ready, run * STEPS + k - 1)
                    dve.tensor_tensor(membrane[:], decayed[:], spikes[:, k - 2, :], ALU.subtract).then_inc(membrane_ready, 1)
                    dve.wait_ge(membrane_ready, first + 1)
                    dve.tensor_scalar(spikes[:, k - 1, :], membrane[:], THRESHOLD, None, ALU.is_gt).then_inc(spike_ready, 1)
                elif (chain, step) == ("e", "count"):
                    dve.wait_ge(misc_full, misc_at(("e.count", n), turn) + 1)
                    dve.wait_ge(stored[n], turn * 16 + 16)
                    dve.scalar_tensor_tensor(out=result[n][:].rearrange("p b c -> p (b c)"), in0=misc[:], scalar=1.0 / STEPS,
                                             in1=x3[:].rearrange("p b c -> p (b c)"), op0=ALU.mult, op1=ALU.add
                                             ).then_inc(misc_free, 1)
                    dve.wait_ge(misc_free, misc_at(("e.count", n), turn) + 1)
                    dve.sem_inc(result_ready, 1)

            dve.memset(minus_ones[:], -1.0).then_inc(stacks_zeroed, 1)
            for n in range(TURN_BATCHES):
                dve.memset(k_stack[n][:].rearrange("p r a q -> p (r a q)").bitcast(F32), 0.0).then_inc(stacks_zeroed, 1)
            dve.memset(zero_rows[:], 0.0).then_inc(v_prepared, 1)
            dve.memset(heads_bank[:], 0.0).then_inc(heads_free, 1)

            dve.wait_ge(w_loaded, 16 * 9)
            dve.tensor_reduce(absmax[:], raw_int4[:], AX_X, ALU.max, apply_absolute_value=True).then_inc(absmax_ready, 1)
            side("q", "norm", 0, None)
            dve.wait_ge(absmax_all, 1)
            dve.tensor_scalar(scale4[:, 1:2], scale4[:, 0:1], 1.0 / INT4_MAX, None, ALU.mult).then_inc(int4_step, 1)
            dve.wait_ge(int4_step, 1)
            dve.reciprocal(inv4[:], scale4[:, 1:2]).then_inc(int4_step, 1)
            dve.wait_ge(int4_step, 2)
            dve.tensor_scalar(int4[:], raw_int4[:], inv4[:], ROUND, ALU.mult, ALU.add).then_inc(int4_step, 1)
            dve.wait_ge(int4_step, 3)
            dve.tensor_scalar(int4[:], int4[:], ROUND, -8.0, ALU.subtract, ALU.max).then_inc(int4_step, 1)
            dve.wait_ge(int4_step, 4)
            dve.tensor_scalar(int4[:], int4[:], 7.0, scale4[:, 1:2], ALU.min, ALU.mult).then_inc(int4_step, 1)
            dve.wait_ge(int4_step, 5)
            dve.wait_ge(int4_ready, 1)
            dve.tensor_tensor(w_linear[:], misc[:, 3 * P:4 * P], int4[:], ALU.add).then_inc(misc_free, 1)
            side("q", "turn", 0, None)
            for n in range(TURN_BATCHES):
                dve.memset(v_ones[n][:, :, :, HEAD_DIM:HEAD_DIM + 1], 1.0).then_inc(v_prepared, 1)
            for s in range(LEAD):
                for u in range(len(units_of(s))):
                    reduce_unit(s, u, 0)
                if s == BLOCKS - 1:
                    split_max(0, 0)

            with dve.Fori(0, TURNS) as turn:
                for s in range(SLOTS):
                    ahead = s + LEAD
                    if ahead < SLOTS:
                        for u in range(len(units_of(ahead))):
                            reduce_unit(ahead, u, turn)
                        if ahead % BLOCKS == BLOCKS - 1:
                            split_max(ahead // BLOCKS, turn)
                    for use in slot_misc(s):
                        if use[0] == "heads":
                            divide_heads(use[1], misc_at(use, turn), turn)
                    for step in SIDE_STEPS[s]:
                        side(*step, turn)
                divide_heads(T_GROUPS - 1, misc_at(("heads", T_GROUPS - 1), turn), turn)
                for k, step in enumerate(TAIL):
                    side(*step, turn)
                    if k < LEAD:
                        for u in range(len(units_of(k))):
                            reduce_unit(k, u, turn + 1)
                        if k == BLOCKS - 1:
                            split_max(0, turn + 1)

        @block.scalar
        def _(act):
            def copy_out(to, use, src=None):
                act.wait_ge(misc_full, use + 1)
                act.copy(to, misc[:] if src is None else src).then_inc(misc_free, 1)

            def exp_tile(slot, t, turn):
                l, kb = layer_of(slot), slot % BLOCKS
                index = TILES_BEFORE[slot] + t
                js = tiles_of(slot)[t]
                width = q_blocks(l, kb)[1]
                per_bank = min(len(js), 512 // width)
                banks = len(js) // per_bank
                src = score_tiles[index % 2][:, 0:banks, 0:per_bank * width]
                to = probs[slot % P_RING][:, js[0] * width:(js[-1] + 1) * width].rearrange("p (a q) -> p a q", a=banks)
                act.wait_ge(tile_full, turn * T_TILES + index + 1)
                if t == 0:
                    act.wait_ge(pv_done, turn * SLOTS + slot + 1)
                act.activation(to, src, ACT.Exp).then_inc(tile_read, 1)

            def take_heads(group, turn):
                act.wait_ge(pv_done, turn * SLOTS + BLOCKS * (group + 1) + P_RING)
                act.copy(heads_t[group % 2][:], heads_bank[:]).then_inc(heads_free, 1)

            def take_max(group, use):
                act.wait_ge(misc_full, use + 1)
                act.copy(max_rows[group % 2][:], misc[0:32, 0:P // 2].bitcast(BF16)).then_inc(misc_free, 1)

            def side(chain, step, n, turn):
                if step not in USES_MISC[chain]:
                    return
                run = run_of(chain, n, turn)
                use = misc_at((chain + "." + step, n), turn)
                l = 0 if chain == "q" else 1
                if step == "turn":
                    copy_out({"q": normed_t["q"], "m": normed_t["m"], "e": heads_all_t}[chain][:], use)
                elif step == "turn2":
                    copy_out(normed_t["m2" if chain == "m" else "e"][:], use)
                elif step in ("q", "k"):
                    act.wait_ge(misc_full, use + 1)
                    if turn is not None:
                        before = {("q", 1): 1, ("m", 0): 1, ("m", 1): 2, ("q", 2): 2}[(chain, n)]
                        other = {("q", 1): 0, ("m", 0): 1, ("m", 1): 0, ("q", 2): 1}[(chain, n)]
                        act.wait_ge(stack_loaded[other], turn * 2 * STACK_DONE + before * STACK_DONE)
                    if l == 0:
                        act.copy(parts[step][:, 0, :], misc[:])
                        act.copy(full[step][:], misc[:]).then_inc(misc_free, 1)
                    else:
                        bias = {"q": bias_q, "k": bias_k}[step]
                        act.activation(parts[step][:, 0, :], misc[:], ACT.Identity, bias=bias[:])
                        act.activation(full[step][:], misc[:], ACT.Identity, bias=bias[:]).then_inc(misc_free, 1)
                elif (chain, step) == ("q", "v"):
                    act.wait_ge(misc_full, use + 1)
                    to = v_ones[n % 2][:].rearrange("p b h c -> p (b h) c")[:, :, 0:HEAD_DIM]
                    act.copy(to, misc[:].rearrange("p (m d) -> p m d", d=HEAD_DIM)).then_inc(misc_free, 1)
                elif step.startswith("fc"):
                    f = int(step[2:])
                    act.wait_ge(misc_full, use + 1)
                    act.activation(relu[:], misc[:], ACT.Relu).then_inc(relu_ready, 1)
                    act.wait_ge(relu_ready, run * CHUNKS + f + 1)
                    act.activation(hidden[:, f, :], relu[:], ACT.Square).then_inc(misc_free, 1)
                elif step == "proj":
                    copy_out(drive[:], use)

            def setup(name):
                use = FIRST_AT[(name, 0)]
                act.wait_ge(misc_full, use + 1)
                q_order, k_order = "c (r a d) -> c d a r", "c (r a d) -> c a d r"

                def put(to, src, order=None, scale=1.0):
                    if order:
                        src = src.rearrange(order, a=2, d=HEAD_DIM)
                        a, b = (HEAD_DIM, 2) if order == q_order else (2, HEAD_DIM)
                        to = to.rearrange("c (x y r) -> c x y r", x=a, y=b)
                    return act.activation(to, src, ACT.Copy, scale=scale)

                if name == "weights_turned":
                    put(uq_t[:], misc[0:LATENT, 0:P])
                    put(o_t[:], misc[:, P:2 * P])
                    last = put(a_t[:], misc[0:RANK, 2 * P:3 * P])
                elif name == "weights_1":
                    put(wq[0][:], misc[:, 0:P], q_order, SCALE)
                    put(qk_t[:], misc[:, P:2 * P])
                    put(v_eff[:], misc[0:LATENT, 2 * P:3 * P]).then_inc(int4_ready, 1)
                    return
                elif name == "weights_2":
                    put(k_eff_t[:], misc[0:LATENT, 0:P])
                    last = put(wv[0][:], misc[:, P:2 * P])
                elif name == "weights_3":
                    last = put(wk[0][:], misc[:, 0:P], k_order)
                elif name == "circulants":
                    put(wq[1][:], misc[:, 0:P], q_order, SCALE)
                    put(wk[1][:], misc[:, P:2 * P], k_order)
                    put(wv[1][:], misc[:, 2 * P:3 * P])
                    last = put(w_out[:], misc[:, 3 * P:4 * P])
                elif name == "bias_columns":
                    put(bias_q[:], misc[:, 0:1], scale=SCALE)
                    last = put(bias_k[:], misc[:, 1:2])
                elif name == "fc_turned":
                    last = put(fc_t[:], misc[:])
                elif name == "proj_turned":
                    last = put(proj_t[:].rearrange("p f c -> p (f c)"), misc[:])
                last.then_inc(misc_free, 1)

            act.sem_inc(tile_read, 2)
            act.sem_inc(pv_done, P_RING)
            act.sem_inc(x2_biased_ready, 1)
            for name in SETUP[:4]:
                setup(name)
            for step in Q_CHAIN:
                side("q", step, 0, None)
            for name in SETUP[4:]:
                setup(name)
            take_max(0, FIRST_AT[("max", 0)])

            with act.Fori(0, TURNS) as turn:
                for s in range(SLOTS):
                    for t in range(len(tiles_of(s))):
                        exp_tile(s, t, turn)
                    if s % BLOCKS == 0 and s > 0:
                        take_heads(s // BLOCKS - 1, turn)
                    for use in slot_misc(s):
                        if use[0] == "max":
                            take_max(use[1], misc_at(use, turn))
                    for step in SIDE_STEPS[s]:
                        side(*step, turn)
                take_heads(T_GROUPS - 1, turn)
                for k, step in enumerate(TAIL):
                    side(*step, turn)
                    if k == LEAD:
                        take_max(T_GROUPS, misc_at(("max", T_GROUPS), turn))


_INS = ['L0_attn_x', 'L0_attn_W_dq', 'L0_attn_W_uq', 'L0_attn_W_dkv', 'L0_attn_W_uk', 'L0_attn_W_uv', 'L0_attn_W_o',
        'L0_ffn_kernel', 'L0_ffn_bias', 'L0_ffn_a', 'L0_ffn_b',
        'L1_attn_wq_c', 'L1_attn_wq_b', 'L1_attn_wk_c', 'L1_attn_wk_b', 'L1_attn_wv_c', 'L1_attn_wv_b',
        'L1_attn_wo_c', 'L1_attn_wo_b', 'L1_ffn_W_fc', 'L1_ffn_W_proj']
_OUTS = [((BATCHES, TOKENS, DIM), 'float32')]


def kernel(**inputs):
    import numpy as _np
    import concourse.bacc as _bacc
    from concourse import mybir as _mybir
    from concourse.bass_utils import run_bass_kernel_spmd as _run

    nc = _bacc.Bacc("TRN2", target_bir_lowering=False, num_devices=1)
    arrays, args = {}, []
    for name in _INS:
        a = _np.ascontiguousarray(inputs[name])
        arrays[f"in_{name}_dram"] = a
        args.append(nc.dram_tensor(f"in_{name}_dram", a.shape, _mybir.dt.from_np(a.dtype), kind="ExternalInput").ap())
    for i, (shape, dtype) in enumerate(_OUTS):
        dt = _mybir.dt.from_np(_np.dtype(dtype))
        args.append(nc.dram_tensor(f"out_{i}_dram", shape, dt, kind="ExternalOutput").ap())
    build_program(nc, *args)
    r = _run(nc, [arrays], core_ids=[0])
    got = tuple(r.results[0][f"out_{i}_dram"] for i in range(len(_OUTS)))
    return got[0]
```

```python
from contextlib import ExitStack

import concourse.bass as bass
from concourse import mybir

F32 = mybir.dt.float32
BF16 = mybir.dt.bfloat16
ALU = mybir.AluOpType
ACT = mybir.ActivationFunctionType
AX_X = mybir.AxisListType.X

P = 128
BATCHES, TOKENS, DIM = 4, 512, 128
HEADS, HEAD_DIM = 16, 8
BLOCKS = TOKENS // P
GROUP = 4
GROUPS = HEADS // GROUP
PAIRS = HEADS // 2
LATENT, RANK = 64, 16
FEATURES = 512
CHUNKS = FEATURES // P
SCALE = float(HEAD_DIM) ** -0.5
LN_EPS = 1e-5
INT4_MAX = 7.0
ROUND = 1.5 * 2.0 ** 23
DECAY, THRESHOLD, STEPS = 0.9, 1.0, 5
MASKED = -1e30

Q_PARTS = (0, 0, 0, 1, 1, 2)
K_PARTS = (0, 1, 2, 0, 1, 0)
TERM_ROWS = 2 * HEAD_DIM
MAX_ROW = len(Q_PARTS) * TERM_ROWS
ROWS = MAX_ROW + 4

PHASES = ((0, 0), (0, 1), (1, 0), (0, 2), (1, 1), (0, 3), (1, 2), (1, 3))
TURNS = 2
PHASE_SLOTS = GROUPS * BLOCKS
SLOTS = len(PHASES) * PHASE_SLOTS
LOOP, LOOP_END, AFTER = (PHASE_SLOTS * p for p in (2, 4, 6))
LEAD = 6

UNITS = {
    0: (((0, (0, 2, 1, 3)), (1, (0, 1)), (1, (2, 3))), ((2, (0,)), (2, (1,)), (2, (2,))),
        ((2, (3,)), (3, (0,)), (3, (1,))), ((3, (2,)), (3, (3,)))),
    1: tuple(tuple((qb, (j,)) for j in range(GROUP)) for qb in range(BLOCKS)),
}
TILES = {
    0: (((0, 1), (2, 3)), ((0, 1), (2, 3)), ((0, 1, 2, 3),), ((0, 1, 2, 3),)),
    1: (((0, 1), (2, 3)),) * BLOCKS,
}


def layer_of(slot):
    return PHASES[slot // PHASE_SLOTS][0]


def stack_of(slot):
    return slot // PHASE_SLOTS % 2


def units_of(slot):
    return UNITS[layer_of(slot)][slot % BLOCKS]


def tiles_of(slot):
    return TILES[layer_of(slot)][slot % BLOCKS]


UNITS_BEFORE = [0]
TILES_BEFORE = [0]
for _s in range(SLOTS):
    UNITS_BEFORE.append(UNITS_BEFORE[-1] + len(units_of(_s)))
    TILES_BEFORE.append(TILES_BEFORE[-1] + len(tiles_of(_s)))
T_SLOTS = LOOP_END - LOOP
T_GROUPS = T_SLOTS // BLOCKS
T_UNITS = UNITS_BEFORE[LOOP_END] - UNITS_BEFORE[LOOP]
T_TILES = TILES_BEFORE[LOOP_END] - TILES_BEFORE[LOOP]
ALL_GROUPS = SLOTS // BLOCKS
P_RING = 2

USES_MISC = {"q": ("turn", "q", "k", "v"), "m": ("turn", "linear", "turn2", "q", "k", "v"),
             "e": ("turn", "out", "turn2", "fc0", "fc1", "fc2", "fc3", "proj", "count")}
Q_CHAIN = ("norm", "turn", "q", "k", "v")
E_CHAIN = ("turn", "out", "turn2", "fc0", "fc1", "fc2", "fc3", "proj", "spike2", "spike3", "spike4",
           "spike5", "count")
LOADS = [("q", 0), ("q", 1), ("m", 0), ("q", 2), ("m", 1), ("q", 3), ("m", 2), ("m", 3)]

Q_EARLY = {"norm": 0, "turn": 1, "q": 2, "k": 3, "v": 5}
Q_LOOP = {"norm": 1, "turn": 2, "q": 3, "k": 4, "v": 5}
M_SHORT = {"add": 1, "norm": 1, "turn": 2, "linear": 3, "turn2": 5, "keep": 6, "q": 6, "k": 7, "v": 9}
M_LOOP = {"add": 1, "norm": 6, "turn": 7, "linear": 9, "turn2": 11, "q": 12, "k": 14}
E_LOOP = {"turn": 2, "out": 3, "turn2": 5, "fc0": 6, "fc1": 7, "fc2": 8, "fc3": 9, "proj": 10, "spike2": 11,
          "spike3": 12, "spike4": 13, "spike5": 14, "count": 15}
LATE = {"v": 1, "keep": 4}


def side_steps():
    at = {s: [] for s in range(SLOTS)}

    def place(chain, batch, phase, steps):
        for name, s in steps.items():
            at[phase * PHASE_SLOTS + s].append((chain, name, batch))

    place("q", 1, 0, Q_EARLY)
    place("m", 0, 1, M_SHORT)
    for k in range(TURNS):
        place("q", k + 2, 2 * k + 2, Q_LOOP)
        place("m", k + 1, 2 * k + 2, M_LOOP)
        place("m", k + 1, 2 * k + 3, {"v": LATE["v"]})
        place("e", k, 2 * k + 3, E_LOOP)
        place("m", k + 1, 2 * k + 3, {"keep": LATE["keep"]})
    place("m", 3, 6, {k: v for k, v in M_SHORT.items() if k != "keep"})
    place("e", 2, 7, E_LOOP)
    place("m", 3, 7, {"keep": LATE["keep"]})
    return at


SIDE_STEPS = side_steps()


def early_misc(slot):
    group, at = divmod(slot, BLOCKS)
    if at == 1 and group > 0:
        return [("heads", group - 1)]
    if at == 2 and group + 1 < ALL_GROUPS:
        return [("max", group + 1)]
    return []


def late_misc(slot):
    return [(c + "." + s, n) for c, s, n in SIDE_STEPS[slot] if s in USES_MISC[c]]


SETUP = ("weights_turned", "weights_1", "weights_2", "weights_3", "circulants", "bias_columns",
         "fc_turned", "proj_turned")
MISC_ORDER = [(s, 0) for s in SETUP[:4]] + [("q." + s, 0) for s in USES_MISC["q"]] \
    + [(s, 0) for s in SETUP[4:]] + [("max", 0)]
MISC_SLOT = []
for _s in range(SLOTS):
    MISC_SLOT.append(len(MISC_ORDER))
    MISC_ORDER += early_misc(_s) + late_misc(_s)
T_MISC = MISC_SLOT[LOOP_END] - MISC_SLOT[LOOP]
MISC_ORDER += [("heads", ALL_GROUPS - 1)] + [("e." + s, 3) for s in USES_MISC["e"]]
MISC_AT = {u: k for k, u in enumerate(MISC_ORDER)}

STACK_DMAS = len(Q_PARTS) + 2 * len(K_PARTS) + 1
STACK_DONE = 16 * STACK_DMAS


def loads_of(chain, batch):
    return [(chain, batch, "zero", 0, 0, 0)] + [
        (chain, batch, t, part, term, half)
        for t, of in (("q", Q_PARTS), ("k", K_PARTS)) for part in range(3)
        for term in range(len(of)) if of[term] == part for half in range(1 if t == "q" else 2)]


def load_steps():
    at = {s: [] for s in range(SLOTS)}
    for (chain, batch), phase, first, each in (
            (("q", 1), 0, 2, 4), (("m", 0), 1, 7, 7), (("q", 2), 2, 3, 4), (("m", 1), 3, 0, 3),
            (("q", 3), 4, 3, 4), (("m", 2), 5, 0, 3), (("m", 3), 6, 7, 7)):
        for k, load in enumerate(loads_of(chain, batch)):
            at[phase * PHASE_SLOTS + first + k // each].append(load)
    return at


LOAD_STEPS = load_steps()


def build_program(nc, x_in, w_dq, w_uq, w_dkv, w_uk, w_uv, w_o, ffn_w, ffn_bias, ffn_a, ffn_b,
                  wq_c, wq_b, wk_c, wk_b, wv_c, wv_b, wo_c, wo_b, w_fc, w_proj, out):
    with ExitStack() as ctx:
        def sb(name, shape, dt=F32):
            return ctx.enter_context(nc.sbuf_tensor(name, shape, dt))

        def sem(name):
            return ctx.enter_context(nc.semaphore(name))

        score_tiles = [ctx.enter_context(nc.psum_tensor(f"score_tile{k}", [P, 2, 512], F32)) for k in range(2)]
        max_banks = [ctx.enter_context(nc.psum_tensor(f"max_bank{k}", [P, 512], F32)) for k in range(2)]
        heads_bank = ctx.enter_context(nc.psum_tensor("heads_bank", [P, TOKENS], F32))
        misc = ctx.enter_context(nc.psum_tensor("misc", [P, 512], F32))

        ident = sb("ident", [P, P])
        ident_bf = sb("ident_bf", [P, P], BF16)
        flip = sb("flip", [P, P])
        mask_qk = sb("mask_qk", [P, P], BF16)
        mask_kq = sb("mask_kq", [P, P], BF16)
        minus_ones = sb("minus_ones", [2, TOKENS], BF16)
        zero_rows = sb("zero_rows", [4, TOKENS], BF16)
        minus_half = sb("minus_half", [P, BLOCKS])
        one = sb("one", [1, 1])

        raw_dq, raw_dkv = sb("raw_dq", [LATENT, P]), sb("raw_dkv", [LATENT, P])
        raw_uq, raw_uk, raw_uv = sb("raw_uq", [P, LATENT]), sb("raw_uk", [P, LATENT]), sb("raw_uv", [P, LATENT])
        raw_o, raw_int4 = sb("raw_o", [P, P]), sb("raw_int4", [P, P])
        raw_a, raw_b = sb("raw_a", [P, RANK]), sb("raw_b", [RANK, P])
        raw_fc, raw_proj = sb("raw_fc", [P, CHUNKS, P]), sb("raw_proj", [P, FEATURES])
        hankel = sb("hankel", [P, 4, P])
        bias_rows = sb("bias_rows", [1, 2, P])
        bias_ordered = sb("bias_ordered", [1, 2, P])
        uq_t, o_t, a_t = sb("uq_t", [LATENT, P]), sb("o_t", [P, P]), sb("a_t", [RANK, P])
        qk_t, v_eff, k_eff_t = sb("qk_t", [P, P]), sb("v_eff", [LATENT, P]), sb("k_eff_t", [LATENT, P])
        wq = [sb(f"wq{l}", [P, P]) for l in range(2)]
        wk = [sb(f"wk{l}", [P, P]) for l in range(2)]
        wv = [sb(f"wv{l}", [P, P]) for l in range(2)]
        w_linear, w_out = sb("w_linear", [P, P]), sb("w_out", [P, P])
        fc_t, proj_t = sb("fc_t", [P, FEATURES]), sb("proj_t", [P, CHUNKS, P])
        bias_q, bias_k = sb("bias_q", [P, 1]), sb("bias_k", [P, 1])
        linear_bias, v_bias, out_bias = (sb(n, [P, P]) for n in ("linear_bias", "v_bias", "out_bias"))
        absmax, scale4, inv4 = sb("absmax", [P, 1]), sb("scale4", [P, 2]), sb("inv4", [P, 1])
        int4 = sb("int4", [P, P])

        q_stack = [sb(f"q_stack{n}", [P, PAIRS, TOKENS], BF16) for n in range(2)]
        k_stack = [sb(f"k_stack{n}", [P, PAIRS, 2, TOKENS], BF16) for n in range(2)]
        v_ones = [sb(f"v_ones{n}", [P, BLOCKS, HEADS, HEAD_DIM + 1]) for n in range(2)]
        heads = [sb(f"heads{n}", [P, BLOCKS, P]) for n in range(2)]
        probs = [sb(f"probs{k}", [P, GROUP * TOKENS]) for k in range(P_RING)]
        row_max = [sb(f"row_max{k}", [P, 2 * 2 * BLOCKS]) for k in range(2)]
        max_parts = [sb(f"max_parts{k}", [P, 2, 2 * 2 * BLOCKS], BF16) for k in range(2)]
        max_rows = [sb(f"max_rows{k}", [32, P], BF16) for k in range(2)]
        heads_t = [sb(f"heads_t{k}", [P, TOKENS]) for k in range(2)]
        inv_sum = sb("inv_sum", [P, BLOCKS, GROUP])

        x_normed, x_added = sb("x_normed", [P, BLOCKS, P]), sb("x_added", [P, BLOCKS, P])
        x1, x1_biased, x2, x2_biased, x3 = (sb(n, [P, BLOCKS, P]) for n in ("x1", "x1_biased", "x2", "x2_biased", "x3"))
        NORMS = ("q", "m", "m2", "e")
        stats = {k: sb("stats_" + k, [P, BLOCKS, 6]) for k in NORMS}
        mean_var = {k: sb("mean_var_" + k, [P, BLOCKS, 2]) for k in NORMS}
        var_eps = {k: sb("var_eps_" + k, [P, BLOCKS]) for k in NORMS}
        rstd = {k: sb("rstd_" + k, [P, BLOCKS]) for k in NORMS}
        normed = {k: sb("normed_" + k, [P, BLOCKS, P]) for k in NORMS}
        normed_t = {k: sb("normed_t_" + k, [P, TOKENS]) for k in NORMS}
        full = {t: sb(f"full_{t}", [P, TOKENS]) for t in "qk"}
        rest = sb("rest", [P, TOKENS])
        parts = {t: sb(f"parts_{t}", [P, 3, TOKENS], BF16) for t in "qk"}
        heads_all_t = sb("heads_all_t", [P, TOKENS])
        relu = sb("relu", [P, TOKENS])
        hidden = sb("hidden", [P, CHUNKS, TOKENS])
        drive, decayed, membrane = sb("drive", [P, TOKENS]), sb("decayed", [P, TOKENS]), sb("membrane", [P, TOKENS])
        spikes = sb("spikes", [P, STEPS, TOKENS], BF16)
        result = sb("result", [P, BLOCKS, P])

        x_normed_loaded, x_added_loaded = sem("x_normed_loaded"), sem("x_added_loaded")
        w_loaded, w1_loaded, doubled = sem("w_loaded"), sem("w1_loaded"), sem("doubled")
        consts_ready, pool_step = sem("consts_ready"), sem("pool_step")
        stacks_zeroed, minus_loaded, v_prepared = sem("stacks_zeroed"), sem("minus_loaded"), sem("v_prepared")
        absmax_ready, absmax_all, int4_step = sem("absmax_ready"), sem("absmax_all"), sem("int4_step")
        int4_ready, bias_ready = sem("int4_ready"), sem("bias_ready")
        misc_full, misc_free = sem("misc_full"), sem("misc_free")
        unit_full, unit_read = sem("unit_full"), sem("unit_read")
        max_high, max_split = sem("max_high"), sem("max_split")
        max_loaded = [sem(f"max_loaded{k}") for k in range(2)]
        tile_full, tile_read = sem("tile_full"), sem("tile_read")
        pv_done, heads_free = sem("pv_done"), sem("heads_free")
        inverted = sem("inverted")
        stack_loaded = [sem(f"stack_loaded{n}") for n in range(2)]
        stats_done = {k: sem("stats_done_" + k) for k in NORMS}
        mean_ready = {k: sem("mean_ready_" + k) for k in NORMS}
        eps_added = {k: sem("eps_added_" + k) for k in NORMS}
        rstd_ready = {k: sem("rstd_ready_" + k) for k in NORMS}
        normed_ready = {k: sem("normed_ready_" + k) for k in NORMS}
        rest_ready = {(l, t): sem(f"rest_ready_{t}{l}") for l in range(2) for t in "qk"}
        middle_ready = {(l, t): sem(f"middle_ready_{t}{l}") for l in range(2) for t in "qk"}
        low_ready = {(l, t): sem(f"low_ready_{t}{l}") for l in range(2) for t in "qk"}
        x1_ready, x1_biased_ready, x2_biased_ready = sem("x1_ready"), sem("x1_biased_ready"), sem("x2_biased_ready")
        relu_ready, spike_ready, decay_ready = sem("relu_ready"), sem("spike_ready"), sem("decay_ready")
        membrane_ready, result_ready = sem("membrane_ready"), sem("result_ready")
        stored = sem("stored")
        waited = sem("waited")

        circ = nc.dram_tensor("circ_twice", (4, 2 * P), F32, kind="Internal")
        circ_ap = circ.ap()

        def misc_at(use, turn):
            return turn * T_MISC + MISC_AT[use]

        def wait(eng, semaphore, value):
            if not isinstance(value, int) or value > 0:
                eng.wait_ge(semaphore, value)

        def wait_apart(eng, semaphore, value):
            eng.wait_ge(semaphore, value)
            eng.sem_inc(waited, 1)

        def q_blocks(l, kb):
            first = kb * P if l == 0 else 0
            return first, TOKENS - first

        def prob_view(k, l, kb, j):
            width = q_blocks(l, kb)[1]
            return probs[k][:, j * width:(j + 1) * width]

        def for_pairs(tile, rows):
            return tile[:].rearrange("p (o q) -> p o q", o=1).to_broadcast([rows, PAIRS, TOKENS])

        block = ctx.enter_context(nc.Block())

        @block.sync
        def _(sp):
            def load_x(x, batch, loaded):
                sp.dma_start(x[:], x_in[batch].rearrange("(b p) c -> p b c", p=P)).then_inc(loaded, 16)

            load_x(x_normed, 0, x_normed_loaded)
            for dst, src in ((raw_uq, w_uq), (raw_o, w_o), (raw_a, ffn_a), (raw_dq, w_dq), (raw_uv, w_uv),
                             (raw_b, ffn_b), (raw_int4, ffn_w), (raw_dkv, w_dkv), (raw_uk, w_uk)):
                sp.dma_start(dst[:], src).then_inc(w_loaded, 16)
            for w, c in enumerate((wq_c, wk_c, wv_c, wo_c)):
                twice = circ_ap[w:w + 1, :].rearrange("o (r n) -> o r n", r=2)
                for r in range(2):
                    sp.dma_start(twice[:, r, :], c.rearrange("(o n) -> o n", o=1)).then_inc(doubled, 16)
            sp.wait_ge(stacks_zeroed, 4)
            for n in range(2):
                for half in range(2):
                    rows = k_stack[n][MAX_ROW + half:ROWS:2, :, half, :]
                    sp.dma_start(rows, for_pairs(minus_ones, 2)).then_inc(minus_loaded, 16)
            sp.sem_inc(stored, 16)

            def load_stack(chain, batch, t, part, term, half, turn):
                number = LOADS.index((chain, batch))
                n, l = number % 2, 0 if chain == "q" else 1
                if t == "zero":
                    if number > 1:
                        sp.wait_ge(tile_full, turn * T_TILES + TILES_BEFORE[(number - 1) * PHASE_SLOTS])
                    sp.dma_start(q_stack[n][MAX_ROW:ROWS, :, :], for_pairs(zero_rows, 4)).then_inc(stack_loaded[n], 16)
                    return
                if part == 0:
                    sp.wait_ge(misc_free, misc_at((chain + "." + t, batch), turn) + 1)
                else:
                    sp.wait_ge((middle_ready, low_ready)[part - 1][(l, t)], turn + batch + 1)
                first = term * TERM_ROWS
                if t == "q":
                    to, src = q_stack[n][first:first + TERM_ROWS, :, :], parts[t][:, part, :]
                else:
                    to = k_stack[n][first + half:first + TERM_ROWS:2, :, half, :]
                    src = parts[t][64 * half:64 * half + 64, part, :]
                sp.dma_start(to, src).then_inc(stack_loaded[n], 16)

            def store_result(batch, turn):
                sp.wait_ge(result_ready, turn + batch + 1)
                dst = out[turn + batch].rearrange("(b p) c -> p b c", p=P)
                sp.dma_start(dst, result[:]).then_inc(stored, 16)

            def load_max_rows(group, turn):
                n, g = group // GROUPS % 2, group % GROUPS
                sp.wait_ge(misc_free, misc_at(("max", group), turn) + 1)
                sp.dma_start(q_stack[n][MAX_ROW:ROWS, 2 * g:2 * g + 2, :].rearrange("p r (b q) -> p (r b) q", b=BLOCKS),
                             max_rows[group % 2][:]).then_inc(max_loaded[group % 2], 16)

            for load in loads_of("q", 0):
                load_stack(*load, 0)
            load_x(x_normed, 1, x_normed_loaded)
            load_x(x_added, 0, x_added_loaded)
            sp.wait_ge(doubled, 16 * 8)
            for w in range(4):
                window = bass.AP(tensor=circ_ap.tensor, offset=w * 2 * P, ap=[[1, P], [1, P]])
                sp.dma_start(hankel[:, w, :], window).then_inc(w1_loaded, 16)
            for k, b in enumerate((wq_b, wk_b)):
                sp.dma_start(bias_rows[:, k, :], b.rearrange("(o n) -> o n", o=1)).then_inc(w1_loaded, 16)
            for dst, src in ((linear_bias, ffn_bias), (v_bias, wv_b), (out_bias, wo_b)):
                sp.dma_start(dst[:], src.rearrange("(o n) -> o n", o=1).to_broadcast([P, P])).then_inc(w1_loaded, 16)
            sp.dma_start(raw_fc[:], w_fc.rearrange("(f p) c -> p f c", p=P)).then_inc(w1_loaded, 16)
            sp.dma_start(raw_proj[:], w_proj).then_inc(w1_loaded, 16)
            load_max_rows(0, 0)

            def slot(s, turn):
                if s == LOOP or s == AFTER:
                    batch = 1 if s == LOOP else 3
                    sp.wait_ge(x1_ready, turn + batch)
                    load_x(x_added, turn + batch, x_added_loaded)
                if s == LOOP:
                    sp.wait_ge(normed_ready["q"], turn + 2)
                    load_x(x_normed, turn + 2, x_normed_loaded)
                for kind, group in early_misc(s):
                    if kind == "max":
                        load_max_rows(group, turn)
                for load in LOAD_STEPS[s]:
                    load_stack(*load, turn)
                for chain, step, batch in SIDE_STEPS[s]:
                    if (chain, step) == ("e", "count"):
                        store_result(batch, turn)

            for s in range(LOOP):
                slot(s, 0)
            with sp.Fori(0, TURNS) as turn:
                for s in range(LOOP, LOOP_END):
                    slot(s, turn)
            for s in range(AFTER, SLOTS):
                slot(s, 0)
            store_result(BATCHES - 1, 0)
            sp.wait_ge(stored, 16 + 16 * BATCHES)

        @block.gpsimd
        def _(pool):
            steps = [0]

            def then_wait(ins):
                steps[0] += 1
                ins.then_inc(pool_step, 1)
                pool.wait_ge(pool_step, steps[0])

            pool.memset(ident[:], 0.0).then_inc(pool_step, 1)
            pool.memset(flip[:], 0.0).then_inc(pool_step, 1)
            pool.memset(mask_qk[:], 0.0).then_inc(pool_step, 1)
            pool.memset(mask_kq[:], 0.0).then_inc(pool_step, 1)
            pool.memset(minus_half[:], -0.5).then_inc(pool_step, 1)
            pool.memset(one[:], 1.0).then_inc(pool_step, 1)
            steps[0] = 6
            pool.wait_ge(pool_step, steps[0])
            then_wait(pool.affine_select(out=ident[:], in_=ident[:], pattern=[[-1, P]], compare_op=ALU.not_equal,
                                         fill=1.0, base=0, channel_multiplier=1))
            then_wait(pool.tensor_copy(ident_bf[:], ident[:]))
            then_wait(pool.affine_select(out=flip[:], in_=flip[:], pattern=[[1, P]], compare_op=ALU.not_equal,
                                         fill=1.0, base=-P, channel_multiplier=1))
            then_wait(pool.affine_select(out=flip[:], in_=flip[:], pattern=[[1, P]], compare_op=ALU.not_equal,
                                         fill=1.0, base=0, channel_multiplier=1))
            pool.affine_select(out=mask_qk[:], in_=mask_qk[:], pattern=[[-1, P]], compare_op=ALU.is_ge,
                               fill=MASKED, base=0, channel_multiplier=1).then_inc(consts_ready, 1)
            pool.affine_select(out=mask_kq[:], in_=mask_kq[:], pattern=[[1, P]], compare_op=ALU.is_ge,
                               fill=MASKED, base=0, channel_multiplier=-1).then_inc(consts_ready, 1)
            pool.wait_ge(absmax_ready, 1)
            pool.partition_all_reduce(scale4[:, 0:1], absmax[:], P, bass.bass_isa.ReduceOp.max).then_inc(absmax_all, 1)

            def inverse_std(k, run):
                wait_apart(pool, mean_ready[k], run + 1)
                pool.tensor_scalar(var_eps[k][:], mean_var[k][:, :, 1], 1.0, LN_EPS, ALU.mult, ALU.add
                                   ).then_inc(eps_added[k], 1)
                pool.wait_ge(eps_added[k], run + 1)
                pool.tensor_tensor(rstd[k][:], var_eps[k][:], minus_half[:], ALU.pow).then_inc(rstd_ready[k], 1)

            def split(l, t, use, run):
                key = (l, t)
                pool.wait_ge(misc_free, use + 1)
                pool.tensor_tensor(rest[:], full[t][:], parts[t][:, 0, :], ALU.subtract
                                   ).then_inc(rest_ready[key], 1)
                wait_apart(pool, rest_ready[key], run + 1)
                pool.tensor_scalar(parts[t][:, 1, :], rest[:], 1.0, 0.0, ALU.mult, ALU.add
                                   ).then_inc(middle_ready[key], 1)
                pool.wait_ge(middle_ready[key], run + 1)
                pool.tensor_tensor(parts[t][:, 2, :], rest[:], parts[t][:, 1, :], ALU.subtract
                                   ).then_inc(low_ready[key], 1)
                pool.wait_ge(low_ready[key], run + 1)

            def rows_of(tile):
                return tile[:].rearrange("p (o c) -> p o c", o=1).to_broadcast([P, BLOCKS, P])

            def side(chain, step, n, turn):
                run = turn + n
                if chain in ("q", "m") and step in ("q", "k"):
                    split(0 if chain == "q" else 1, step, misc_at((chain + "." + step, n), turn), run)
                elif (chain, step) in (("q", "norm"), ("m", "norm")):
                    inverse_std(chain, run)
                elif (chain, step) == ("m", "add"):
                    phase = PHASES.index((0, n))
                    pool.wait_ge(misc_free, misc_at(("heads", GROUPS * (phase + 1) - 1), turn) + 1)
                    pool.wait_ge(x_added_loaded, turn * 16 + 16 * (n + 1))
                    pool.tensor_tensor(x1[:], x_added[:], heads[phase % 2][:], ALU.add).then_inc(x1_ready, 1)
                    pool.wait_ge(x1_ready, run + 1)
                    pool.tensor_tensor(x1_biased[:], x1[:], rows_of(linear_bias), ALU.add).then_inc(x1_biased_ready, 1)
                elif (chain, step) == ("m", "linear"):
                    inverse_std("m2", run)
                elif (chain, step) == ("m", "keep"):
                    if n > 0:
                        pool.wait_ge(misc_free, misc_at(("e.out", n - 1), turn) + 1)
                    pool.tensor_tensor(x2_biased[:], x2[:], rows_of(out_bias), ALU.add).then_inc(x2_biased_ready, 1)
                elif (chain, step) == ("e", "out"):
                    inverse_std("e", run)

            for step in Q_CHAIN:
                side("q", step, 0, 0)
            pool.wait_ge(w1_loaded, 16 * 11)
            for k, (a, b, order) in enumerate(((HEAD_DIM, 2, "o (r a d) -> o d a r"), (2, HEAD_DIM, "o (r a d) -> o a d r"))):
                pool.tensor_copy(bias_ordered[:, k, :].rearrange("o (x y r) -> o x y r", x=a, y=b),
                                 bias_rows[:, k, :].rearrange(order, a=2, d=HEAD_DIM)).then_inc(bias_ready, 1)
            def slot(s, turn):
                for step in SIDE_STEPS[s]:
                    side(*step, turn)

            for s in range(LOOP):
                slot(s, 0)
            with pool.Fori(0, TURNS) as turn:
                for s in range(LOOP, LOOP_END):
                    slot(s, turn)
            for s in range(AFTER, SLOTS):
                slot(s, 0)
            for step in E_CHAIN:
                side("e", step, BATCHES - 1, 0)

        @block.tensor
        def _(pe):
            def open_misc(use):
                wait(pe, misc_free, use)

            def turn_blocks(src):
                for b in range(BLOCKS):
                    last = pe.transpose(misc[:, b * P:(b + 1) * P], src[:, b, :], ident[:])
                last.then_inc(misc_full, 1)

            def by_token(src_t, w):
                for b in range(BLOCKS):
                    last = pe.matmul(misc[:, b * P:(b + 1) * P], src_t[:, b * P:(b + 1) * P], w[:], start=True, stop=True)
                last.then_inc(misc_full, 1)

            def side(chain, step, n, turn):
                if step not in USES_MISC[chain]:
                    return
                run = turn + n
                l = 0 if chain == "q" else 1
                k2 = {"q": "q", "m": "m2"}.get(chain)
                open_misc(misc_at((chain + "." + step, n), turn))
                if step == "turn" and chain != "e":
                    pe.wait_ge(normed_ready[chain], run + 1)
                    turn_blocks(normed[chain])
                elif step == "turn":
                    turn_blocks(heads[PHASES.index((1, n)) % 2])
                elif step == "turn2":
                    k = "m2" if chain == "m" else "e"
                    pe.wait_ge(normed_ready[k], run + 1)
                    turn_blocks(normed[k])
                elif step in ("q", "k"):
                    w = (wq if step == "q" else wk)[l]
                    pe.matmul(misc[:], w[:], normed_t[k2][:], start=True, stop=True).then_inc(misc_full, 1)
                elif step == "v":
                    by_token(normed_t[k2], wv[l])
                elif step == "linear":
                    by_token(normed_t["m"], w_linear)
                elif step == "out":
                    by_token(heads_all_t, w_out)
                elif step.startswith("fc"):
                    f = int(step[2:])
                    pe.matmul(misc[:], fc_t[:, f * P:(f + 1) * P], normed_t["e"][:], start=True, stop=True
                              ).then_inc(misc_full, 1)
                elif step == "proj":
                    for f in range(CHUNKS):
                        last = pe.matmul(misc[:], proj_t[:, f, :], hidden[:, f, :], start=(f == 0), stop=(f == CHUNKS - 1))
                    last.then_inc(misc_full, 1)
                elif step == "count":
                    pe.wait_ge(spike_ready, turn * STEPS + (n + 1) * STEPS)
                    for b in range(BLOCKS):
                        for k in range(STEPS):
                            last = pe.matmul(misc[:, b * P:(b + 1) * P], spikes[:, k, b * P:(b + 1) * P], ident_bf[:],
                                             start=(k == 0), stop=(k == STEPS - 1))
                    last.then_inc(misc_full, 1)

            def score_unit(slot, u, turn):
                l, n = layer_of(slot), stack_of(slot)
                g = slot // BLOCKS % GROUPS
                qb, js = units_of(slot)[u]
                count = turn * T_UNITS + UNITS_BEFORE[slot] + u
                bank = max_banks[(UNITS_BEFORE[slot] + u) % 2]
                if slot % PHASE_SLOTS == 0 and u == 0:
                    pe.wait_ge(stack_loaded[n], turn * STACK_DONE + (slot // (2 * PHASE_SLOTS) + 1) * STACK_DONE)
                wait(pe, unit_read, count - 1)
                width = (qb + 1) * P if l == 0 else TOKENS
                for k, j in enumerate(js):
                    pair, half = 2 * g + j // 2, j % 2
                    last = pe.matmul(bank[:, k * width:(k + 1) * width], q_stack[n][0:ROWS, pair, qb * P:(qb + 1) * P],
                                     k_stack[n][0:ROWS, pair, half, 0:width], start=True, stop=(l == 1))
                    if l == 0:
                        last = pe.matmul(bank[:, (k + 1) * width - P:(k + 1) * width], ident_bf[:], mask_qk[:],
                                         start=False, stop=True)
                last.then_inc(unit_full, 1)

            def turn_max(group, turn):
                use = misc_at(("max", group), turn)
                open_misc(use)
                pe.wait_ge(max_split, turn * T_GROUPS + group + 1)
                pe.transpose(misc[0:32, 0:P // 2].bitcast(BF16), max_parts[group % 2][:].rearrange("p a c -> p (a c)"),
                             ident_bf[:]).then_inc(misc_full, 1)

            def turn_heads(group, turn):
                use = misc_at(("heads", group), turn)
                open_misc(use)
                pe.wait_ge(heads_free, turn * T_GROUPS + group + 2)
                for b in range(BLOCKS):
                    last = pe.transpose(misc[:, b * P:(b + 1) * P], heads_t[group % 2][:, b * P:(b + 1) * P], ident[:])
                last.then_inc(misc_full, 1)

            def score_tile(slot, t, turn):
                l, n = layer_of(slot), stack_of(slot)
                group, kb = divmod(slot, BLOCKS)
                g = group % GROUPS
                index = TILES_BEFORE[slot] + t
                tile = score_tiles[index % 2]
                if kb == 0 and t == 0:
                    pe.wait_ge(max_loaded[group % 2], turn * (16 * T_GROUPS // 2) + 16 * (group // 2 + 1))
                pe.wait_ge(tile_read, turn * T_TILES + index + 1)
                js = tiles_of(slot)[t]
                first, width = q_blocks(l, kb)
                per_bank = min(len(js), 512 // width)
                for k, j in enumerate(js):
                    pair, half = 2 * g + j // 2, j % 2
                    at = tile[:, k // per_bank, (k % per_bank) * width:(k % per_bank + 1) * width]
                    last = pe.matmul(at, k_stack[n][0:ROWS, pair, half, kb * P:(kb + 1) * P],
                                     q_stack[n][0:ROWS, pair, first:TOKENS], start=True, stop=(l == 1))
                    if l == 0:
                        last = pe.matmul(at[:, 0:P], ident_bf[:], mask_kq[:], start=False, stop=True)
                last.then_inc(tile_full, 1)

            def times_v(slot, js, turn):
                l, n = layer_of(slot), stack_of(slot)
                group, kb = divmod(slot, BLOCKS)
                first, width = q_blocks(l, kb)
                if js[0] == 0:
                    pe.wait_ge(tile_read, turn * T_TILES + TILES_BEFORE[slot + 1] + 2)
                    if kb == 0:
                        pe.wait_ge(heads_free, turn * T_GROUPS + group + 1)
                for j in js:
                    h = GROUP * (group % GROUPS) + j
                    last = pe.matmul(heads_bank[32 * j:32 * j + HEAD_DIM + 1, first:TOKENS], v_ones[n][:, kb, h, :],
                                     prob_view(slot % P_RING, l, kb, j), start=(kb == 0), stop=(kb == BLOCKS - 1),
                                     skip_group_check=True, tile_position=(0, 32 * j))
                if js[-1] == GROUP - 1:
                    last.then_inc(pv_done, 1)

            def setup(name):
                open_misc(misc_at((name, 0), 0))
                if name == "weights_turned":
                    pe.wait_ge(consts_ready, 2)
                    pe.wait_ge(w_loaded, 16 * 9)
                    pe.transpose(misc[0:LATENT, 0:P], raw_uq[:], ident[:])
                    pe.transpose(misc[:, P:2 * P], raw_o[:], ident[:])
                    last = pe.transpose(misc[0:RANK, 2 * P:3 * P], raw_a[:], ident[:])
                elif name == "weights_1":
                    pe.matmul(misc[:, 0:P], raw_dq[:], uq_t[:], start=True, stop=True)
                    pe.matmul(misc[:, P:2 * P], uq_t[:], raw_dq[:], start=True, stop=True)
                    pe.matmul(misc[0:LATENT, 2 * P:3 * P], raw_uv[:], o_t[:], start=True, stop=True)
                    last = pe.matmul(misc[:, 3 * P:4 * P], a_t[:], raw_b[:], start=True, stop=True)
                elif name == "weights_2":
                    pe.matmul(misc[0:LATENT, 0:P], raw_uk[:], qk_t[:], start=True, stop=True)
                    last = pe.matmul(misc[:, P:2 * P], raw_dkv[:], v_eff[:], start=True, stop=True)
                elif name == "weights_3":
                    last = pe.matmul(misc[:, 0:P], raw_dkv[:], k_eff_t[:], start=True, stop=True)
                elif name == "circulants":
                    pe.wait_ge(w1_loaded, 16 * 11)
                    for w in range(4):
                        last = pe.matmul(misc[:, w * P:(w + 1) * P], flip[:], hankel[:, w, :], start=True, stop=True)
                elif name == "bias_columns":
                    pe.wait_ge(bias_ready, 2)
                    for k in range(2):
                        last = pe.matmul(misc[:, k:k + 1], bias_ordered[:, k, :], one[:], start=True, stop=True)
                elif name == "fc_turned":
                    for f in range(CHUNKS):
                        last = pe.transpose(misc[:, f * P:(f + 1) * P], raw_fc[:, f, :], ident[:])
                elif name == "proj_turned":
                    for f in range(CHUNKS):
                        last = pe.transpose(misc[:, f * P:(f + 1) * P], raw_proj[:, f * P:(f + 1) * P], ident[:])
                last.then_inc(misc_full, 1)

            for name in SETUP[:4]:
                setup(name)
            for step in Q_CHAIN:
                side("q", step, 0, 0)
            for name in SETUP[4:]:
                setup(name)
            pe.wait_ge(minus_loaded, 16 * 4)
            pe.wait_ge(v_prepared, 2)
            for s in range(LEAD):
                for u in range(len(units_of(s))):
                    score_unit(s, u, 0)
            turn_max(0, 0)

            def slot(s, turn):
                todo = list(range(len(units_of(s + LEAD)))) if s + LEAD < SLOTS else []

                def some_units(k):
                    for u in todo[:k]:
                        score_unit(s + LEAD, u, turn)
                    del todo[:k]

                score_tile(s, 0, turn)
                some_units(1)
                for kind, group in early_misc(s):
                    (turn_max if kind == "max" else turn_heads)(group, turn)
                if s > 0:
                    times_v(s - 1, (0, 1, 2, 3), turn)
                some_units(1)
                if len(tiles_of(s)) > 1:
                    score_tile(s, 1, turn)
                some_units(len(todo))
                for step in SIDE_STEPS[s]:
                    side(*step, turn)

            for s in range(LOOP):
                slot(s, 0)
            with pe.Fori(0, TURNS) as turn:
                for s in range(LOOP, LOOP_END):
                    slot(s, turn)
            for s in range(AFTER, SLOTS):
                slot(s, 0)
            times_v(SLOTS - 1, (0, 1, 2, 3), 0)
            turn_heads(ALL_GROUPS - 1, 0)
            for step in E_CHAIN:
                side("e", step, BATCHES - 1, 0)

        @block.vector
        def _(dve):
            def max_view(group):
                return row_max[group % 2][:].rearrange("p (a r b) -> p a r b", a=2, r=2)

            def reduce_unit(slot, u, turn):
                l, group = layer_of(slot), slot // BLOCKS
                qb, js = units_of(slot)[u]
                count = turn * T_UNITS + UNITS_BEFORE[slot] + u
                bank = max_banks[(UNITS_BEFORE[slot] + u) % 2]
                width = (qb + 1) * P if l == 0 else TOKENS
                to = max_view(group)
                scores = bank[:, 0:len(js) * width]
                if len(js) == 4:
                    to, scores = to[:, :, :, qb], scores.rearrange("p (a r q) -> p a r q", a=2, r=2)
                elif len(js) == 2:
                    to, scores = to[:, :, js[0] // 2, qb], scores.rearrange("p (a q) -> p a q", a=2)
                else:
                    to = to[:, js[0] % 2, js[0] // 2, qb:qb + 1]
                dve.wait_ge(unit_full, count + 1)
                dve.tensor_reduce(to, scores, AX_X, ALU.max).then_inc(unit_read, 1)

            def split_max(group, turn):
                dve.wait_ge(unit_read, turn * T_UNITS + UNITS_BEFORE[BLOCKS * (group + 1)])
                dve.tensor_copy(max_parts[group % 2][:, 0, :], row_max[group % 2][:]).then_inc(max_high, 1)
                dve.wait_ge(max_high, turn * T_GROUPS + group + 1)
                dve.tensor_tensor(max_parts[group % 2][:, 1, :], row_max[group % 2][:], max_parts[group % 2][:, 0, :],
                                  ALU.subtract).then_inc(max_split, 1)

            def divide_heads(group, turn):
                use = misc_at(("heads", group), turn)
                n, g = group // GROUPS % 2, group % GROUPS
                view = misc[:].rearrange("p (b j c) -> p b j c", b=BLOCKS, j=GROUP)
                dve.wait_ge(misc_full, use + 1)
                dve.reciprocal(inv_sum[:], view[:, :, :, HEAD_DIM]).then_inc(inverted, 1)
                dve.wait_ge(inverted, turn * T_GROUPS + group + 1)
                to = heads[n][:, :, g * 32:(g + 1) * 32].rearrange("p b (j d) -> p b j d", j=GROUP)
                inv = inv_sum[:].rearrange("p b (j o) -> p b j o", o=1).to_broadcast([P, BLOCKS, GROUP, HEAD_DIM])
                dve.tensor_tensor(to, view[:, :, :, 0:HEAD_DIM], inv, ALU.mult).then_inc(misc_free, 1)

            def statistics(k, x, run):
                for b in range(BLOCKS):
                    last = dve.bn_stats(stats[k][:, b, :], x[:, b, :])
                last.then_inc(stats_done[k], 1)
                wait_apart(dve, stats_done[k], run + 1)
                for b in range(BLOCKS):
                    last = dve.bn_aggr(mean_var[k][:, b, :], stats[k][:, b, :])
                last.then_inc(mean_ready[k], 1)

            def normalise(k, x, run):
                dve.wait_ge(rstd_ready[k], run + 1)
                for b in range(BLOCKS):
                    last = dve.tensor_scalar(normed[k][:, b, :], x[:, b, :], mean_var[k][:, b, 0:1], rstd[k][:, b:b + 1],
                                             ALU.subtract, ALU.mult)
                last.then_inc(normed_ready[k], 1)

            misc_blocks = misc[:].rearrange("p (b c) -> p b c", b=BLOCKS)

            def side(chain, step, n, turn):
                run = turn + n
                if (chain, step) == ("q", "norm"):
                    dve.wait_ge(x_normed_loaded, turn * 16 + 16 * (n + 1))
                    statistics("q", x_normed, run)
                elif (chain, step) == ("q", "turn"):
                    normalise("q", x_normed, run)
                elif (chain, step) == ("m", "norm"):
                    dve.wait_ge(x1_ready, run + 1)
                    statistics("m", x1, run)
                elif (chain, step) == ("m", "turn"):
                    normalise("m", x1, run)
                elif (chain, step) == ("m", "linear"):
                    dve.wait_ge(misc_full, misc_at(("m.linear", n), turn) + 1)
                    dve.wait_ge(x1_biased_ready, run + 1)
                    if n > 0:
                        dve.wait_ge(x2_biased_ready, turn + n)
                    dve.tensor_tensor(x2[:], misc_blocks, x1_biased[:], ALU.add).then_inc(misc_free, 1)
                    dve.wait_ge(misc_free, misc_at(("m.linear", n), turn) + 1)
                    statistics("m2", x2, run)
                elif (chain, step) == ("m", "turn2"):
                    normalise("m2", x2, run)
                elif (chain, step) == ("m", "v"):
                    dve.wait_ge(misc_full, misc_at(("m.v", n), turn) + 1)
                    to = v_ones[LOADS.index(("m", n)) % 2][:].rearrange("p b h c -> p (b h) c")[:, :, 0:HEAD_DIM]
                    dve.tensor_tensor(to, misc[:].rearrange("p (m d) -> p m d", d=HEAD_DIM),
                                      v_bias[:].rearrange("p (o c) -> p o c", o=1).to_broadcast([P, BLOCKS, P]),
                                      ALU.add).then_inc(misc_free, 1)
                elif (chain, step) == ("e", "out"):
                    dve.wait_ge(misc_full, misc_at(("e.out", n), turn) + 1)
                    dve.wait_ge(x2_biased_ready, run + 1)
                    dve.tensor_tensor(x3[:], misc_blocks, x2_biased[:], ALU.add).then_inc(misc_free, 1)
                    dve.wait_ge(misc_free, misc_at(("e.out", n), turn) + 1)
                    statistics("e", x3, run)
                elif (chain, step) == ("e", "turn2"):
                    normalise("e", x3, run)
                elif chain == "e" and step.startswith("spike"):
                    k = int(step[5:])
                    first = turn * (STEPS - 1) + n * (STEPS - 1) + k - 2
                    mem = drive if k == 2 else membrane
                    if k == 2:
                        dve.wait_ge(misc_free, misc_at(("e.proj", n), turn) + 1)
                        dve.tensor_scalar(spikes[:, 0, :], drive[:], THRESHOLD, None, ALU.is_gt).then_inc(spike_ready, 1)
                    dve.scalar_tensor_tensor(out=decayed[:], in0=mem[:], scalar=DECAY, in1=drive[:],
                                             op0=ALU.mult, op1=ALU.add).then_inc(decay_ready, 1)
                    dve.wait_ge(decay_ready, first + 1)
                    dve.wait_ge(spike_ready, turn * STEPS + n * STEPS + k - 1)
                    dve.tensor_tensor(membrane[:], decayed[:], spikes[:, k - 2, :], ALU.subtract).then_inc(membrane_ready, 1)
                    dve.wait_ge(membrane_ready, first + 1)
                    dve.tensor_scalar(spikes[:, k - 1, :], membrane[:], THRESHOLD, None, ALU.is_gt).then_inc(spike_ready, 1)
                elif (chain, step) == ("e", "count"):
                    dve.wait_ge(misc_full, misc_at(("e.count", n), turn) + 1)
                    dve.wait_ge(stored, turn * 16 + 16 * (n + 1))
                    dve.scalar_tensor_tensor(out=result[:].rearrange("p b c -> p (b c)"), in0=misc[:], scalar=1.0 / STEPS,
                                             in1=x3[:].rearrange("p b c -> p (b c)"), op0=ALU.mult, op1=ALU.add
                                             ).then_inc(misc_free, 1)
                    dve.wait_ge(misc_free, misc_at(("e.count", n), turn) + 1)
                    dve.sem_inc(result_ready, 1)

            dve.memset(minus_ones[:], -1.0).then_inc(stacks_zeroed, 1)
            dve.memset(zero_rows[:], 0.0).then_inc(stacks_zeroed, 1)
            for n in range(2):
                dve.memset(k_stack[n][:].rearrange("p r a q -> p (r a q)").bitcast(F32), 0.0).then_inc(stacks_zeroed, 1)
            dve.memset(heads_bank[:], 0.0).then_inc(heads_free, 1)

            dve.wait_ge(w_loaded, 16 * 9)
            dve.tensor_reduce(absmax[:], raw_int4[:], AX_X, ALU.max, apply_absolute_value=True).then_inc(absmax_ready, 1)
            side("q", "norm", 0, 0)
            dve.wait_ge(absmax_all, 1)
            dve.tensor_scalar(scale4[:, 1:2], scale4[:, 0:1], 1.0 / INT4_MAX, None, ALU.mult).then_inc(int4_step, 1)
            dve.wait_ge(int4_step, 1)
            dve.reciprocal(inv4[:], scale4[:, 1:2]).then_inc(int4_step, 1)
            dve.wait_ge(int4_step, 2)
            dve.tensor_scalar(int4[:], raw_int4[:], inv4[:], ROUND, ALU.mult, ALU.add).then_inc(int4_step, 1)
            dve.wait_ge(int4_step, 3)
            dve.tensor_scalar(int4[:], int4[:], ROUND, -8.0, ALU.subtract, ALU.max).then_inc(int4_step, 1)
            dve.wait_ge(int4_step, 4)
            dve.tensor_scalar(int4[:], int4[:], 7.0, scale4[:, 1:2], ALU.min, ALU.mult).then_inc(int4_step, 1)
            dve.wait_ge(int4_step, 5)
            dve.wait_ge(int4_ready, 1)
            dve.tensor_tensor(w_linear[:], misc[:, 3 * P:4 * P], int4[:], ALU.add).then_inc(misc_free, 1)
            side("q", "turn", 0, 0)
            for n in range(2):
                dve.memset(v_ones[n][:, :, :, HEAD_DIM:HEAD_DIM + 1], 1.0).then_inc(v_prepared, 1)
            for s in range(LEAD):
                for u in range(len(units_of(s))):
                    reduce_unit(s, u, 0)
                if s == BLOCKS - 1:
                    split_max(0, 0)

            def slot(s, turn):
                ahead = s + LEAD
                todo = [u for u in range(len(units_of(ahead)))] if ahead < SLOTS else []
                for u in todo[:1]:
                    reduce_unit(ahead, u, turn)
                for kind, group in early_misc(s):
                    if kind == "heads":
                        divide_heads(group, turn)
                for u in todo[1:]:
                    reduce_unit(ahead, u, turn)
                if ahead < SLOTS and ahead % BLOCKS == BLOCKS - 1:
                    split_max(ahead // BLOCKS, turn)
                for step in SIDE_STEPS[s]:
                    side(*step, turn)

            for s in range(LOOP):
                slot(s, 0)
            with dve.Fori(0, TURNS) as turn:
                for s in range(LOOP, LOOP_END):
                    slot(s, turn)
            for s in range(AFTER, SLOTS):
                slot(s, 0)
            divide_heads(ALL_GROUPS - 1, 0)
            for step in E_CHAIN:
                side("e", step, BATCHES - 1, 0)

        @block.scalar
        def _(act):
            def copy_out(to, use, src=None):
                act.wait_ge(misc_full, use + 1)
                act.copy(to, misc[:] if src is None else src).then_inc(misc_free, 1)

            def exp_tile(slot, t, turn):
                l, kb = layer_of(slot), slot % BLOCKS
                index = TILES_BEFORE[slot] + t
                js = tiles_of(slot)[t]
                width = q_blocks(l, kb)[1]
                per_bank = min(len(js), 512 // width)
                banks = len(js) // per_bank
                src = score_tiles[index % 2][:, 0:banks, 0:per_bank * width]
                to = probs[slot % P_RING][:, js[0] * width:(js[-1] + 1) * width].rearrange("p (a q) -> p a q", a=banks)
                act.wait_ge(tile_full, turn * T_TILES + index + 1)
                if t == 0:
                    act.wait_ge(pv_done, turn * T_SLOTS + slot + 1)
                act.activation(to, src, ACT.Exp).then_inc(tile_read, 1)

            def take_heads(group, turn):
                act.wait_ge(pv_done, turn * T_SLOTS + BLOCKS * (group + 1) + P_RING)
                act.copy(heads_t[group % 2][:], heads_bank[:]).then_inc(heads_free, 1)

            def take_max(group, turn):
                act.wait_ge(misc_full, misc_at(("max", group), turn) + 1)
                act.copy(max_rows[group % 2][:], misc[0:32, 0:P // 2].bitcast(BF16)).then_inc(misc_free, 1)

            def side(chain, step, n, turn):
                if step not in USES_MISC[chain]:
                    return
                run = turn + n
                use = misc_at((chain + "." + step, n), turn)
                l = 0 if chain == "q" else 1
                if step == "turn":
                    copy_out({"q": normed_t["q"], "m": normed_t["m"], "e": heads_all_t}[chain][:], use)
                elif step == "turn2":
                    copy_out(normed_t["m2" if chain == "m" else "e"][:], use)
                elif step in ("q", "k"):
                    act.wait_ge(misc_full, use + 1)
                    number = LOADS.index((chain, n))
                    if number > 0:
                        act.wait_ge(stack_loaded[(number - 1) % 2], turn * STACK_DONE + ((number - 1) // 2 + 1) * STACK_DONE)
                    if l == 0:
                        act.copy(parts[step][:, 0, :], misc[:])
                        act.copy(full[step][:], misc[:]).then_inc(misc_free, 1)
                    else:
                        bias = {"q": bias_q, "k": bias_k}[step]
                        act.activation(parts[step][:, 0, :], misc[:], ACT.Identity, bias=bias[:])
                        act.activation(full[step][:], misc[:], ACT.Identity, bias=bias[:]).then_inc(misc_free, 1)
                elif (chain, step) == ("q", "v"):
                    act.wait_ge(misc_full, use + 1)
                    to = v_ones[LOADS.index(("q", n)) % 2][:].rearrange("p b h c -> p (b h) c")[:, :, 0:HEAD_DIM]
                    act.copy(to, misc[:].rearrange("p (m d) -> p m d", d=HEAD_DIM)).then_inc(misc_free, 1)
                elif step.startswith("fc"):
                    f = int(step[2:])
                    act.wait_ge(misc_full, use + 1)
                    act.activation(relu[:], misc[:], ACT.Relu).then_inc(relu_ready, 1)
                    act.wait_ge(relu_ready, turn * CHUNKS + n * CHUNKS + f + 1)
                    act.activation(hidden[:, f, :], relu[:], ACT.Square).then_inc(misc_free, 1)
                elif step == "proj":
                    copy_out(drive[:], use)

            def setup(name):
                use = misc_at((name, 0), 0)
                act.wait_ge(misc_full, use + 1)
                q_order, k_order = "c (r a d) -> c d a r", "c (r a d) -> c a d r"

                def put(to, src, order=None, scale=1.0):
                    if order:
                        src = src.rearrange(order, a=2, d=HEAD_DIM)
                        a, b = (HEAD_DIM, 2) if order == q_order else (2, HEAD_DIM)
                        to = to.rearrange("c (x y r) -> c x y r", x=a, y=b)
                    return act.activation(to, src, ACT.Copy, scale=scale)

                if name == "weights_turned":
                    put(uq_t[:], misc[0:LATENT, 0:P])
                    put(o_t[:], misc[:, P:2 * P])
                    last = put(a_t[:], misc[0:RANK, 2 * P:3 * P])
                elif name == "weights_1":
                    put(wq[0][:], misc[:, 0:P], q_order, SCALE)
                    put(qk_t[:], misc[:, P:2 * P])
                    put(v_eff[:], misc[0:LATENT, 2 * P:3 * P]).then_inc(int4_ready, 1)
                    return
                elif name == "weights_2":
                    put(k_eff_t[:], misc[0:LATENT, 0:P])
                    last = put(wv[0][:], misc[:, P:2 * P])
                elif name == "weights_3":
                    last = put(wk[0][:], misc[:, 0:P], k_order)
                elif name == "circulants":
                    put(wq[1][:], misc[:, 0:P], q_order, SCALE)
                    put(wk[1][:], misc[:, P:2 * P], k_order)
                    put(wv[1][:], misc[:, 2 * P:3 * P])
                    last = put(w_out[:], misc[:, 3 * P:4 * P])
                elif name == "bias_columns":
                    put(bias_q[:], misc[:, 0:1], scale=SCALE)
                    last = put(bias_k[:], misc[:, 1:2])
                elif name == "fc_turned":
                    last = put(fc_t[:], misc[:])
                elif name == "proj_turned":
                    last = put(proj_t[:].rearrange("p f c -> p (f c)"), misc[:])
                last.then_inc(misc_free, 1)

            act.sem_inc(tile_read, 2)
            act.sem_inc(pv_done, P_RING)
            for name in SETUP[:4]:
                setup(name)
            for step in Q_CHAIN:
                side("q", step, 0, 0)
            for name in SETUP[4:]:
                setup(name)
            take_max(0, 0)

            def slot(s, turn):
                exp_tile(s, 0, turn)
                for kind, group in early_misc(s):
                    if kind == "max":
                        take_max(group, turn)
                if len(tiles_of(s)) > 1:
                    exp_tile(s, 1, turn)
                if s % BLOCKS == 0 and s > 0:
                    take_heads(s // BLOCKS - 1, turn)
                for step in SIDE_STEPS[s]:
                    side(*step, turn)

            for s in range(LOOP):
                slot(s, 0)
            with act.Fori(0, TURNS) as turn:
                for s in range(LOOP, LOOP_END):
                    slot(s, turn)
            for s in range(AFTER, SLOTS):
                slot(s, 0)
            take_heads(ALL_GROUPS - 1, 0)
            for step in E_CHAIN:
                side("e", step, BATCHES - 1, 0)


_INS = ['L0_attn_x', 'L0_attn_W_dq', 'L0_attn_W_uq', 'L0_attn_W_dkv', 'L0_attn_W_uk', 'L0_attn_W_uv', 'L0_attn_W_o',
        'L0_ffn_kernel', 'L0_ffn_bias', 'L0_ffn_a', 'L0_ffn_b',
        'L1_attn_wq_c', 'L1_attn_wq_b', 'L1_attn_wk_c', 'L1_attn_wk_b', 'L1_attn_wv_c', 'L1_attn_wv_b',
        'L1_attn_wo_c', 'L1_attn_wo_b', 'L1_ffn_W_fc', 'L1_ffn_W_proj']
_OUTS = [((BATCHES, TOKENS, DIM), 'float32')]


def kernel(**inputs):
    import numpy as _np
    import concourse.bacc as _bacc
    from concourse import mybir as _mybir
    from concourse.bass_utils import run_bass_kernel_spmd as _run

    nc = _bacc.Bacc("TRN2", target_bir_lowering=False, num_devices=1)
    arrays, args = {}, []
    for name in _INS:
        a = _np.ascontiguousarray(inputs[name])
        arrays[f"in_{name}_dram"] = a
        args.append(nc.dram_tensor(f"in_{name}_dram", a.shape, _mybir.dt.from_np(a.dtype), kind="ExternalInput").ap())
    for i, (shape, dtype) in enumerate(_OUTS):
        dt = _mybir.dt.from_np(_np.dtype(dtype))
        args.append(nc.dram_tensor(f"out_{i}_dram", shape, dt, kind="ExternalOutput").ap())
    build_program(nc, *args)
    r = _run(nc, [arrays], core_ids=[0])
    got = tuple(r.results[0][f"out_{i}_dram"] for i in range(len(_OUTS)))
    return got[0]
```

```python
from contextlib import ExitStack

import concourse.bass as bass
from concourse import mybir

F32 = mybir.dt.float32
BF16 = mybir.dt.bfloat16
ALU = mybir.AluOpType
ACT = mybir.ActivationFunctionType
AX_X = mybir.AxisListType.X

P = 128
BATCHES, TOKENS, DIM = 4, 512, 128
HEADS, HEAD_DIM = 16, 8
BLOCKS = TOKENS // P
GROUP = 4
GROUPS = HEADS // GROUP
PAIRS = HEADS // 2
LATENT, RANK = 64, 16
FEATURES = 512
CHUNKS = FEATURES // P
SCALE = float(HEAD_DIM) ** -0.5
LN_EPS = 1e-5
INT4_MAX = 7.0
ROUND = 1.5 * 2.0 ** 23
DECAY, THRESHOLD, STEPS = 0.9, 1.0, 5
MASKED = -1e30

Q_PARTS = (0, 0, 0, 1, 1, 2)
K_PARTS = (0, 1, 2, 0, 1, 0)
TERM_ROWS = 2 * HEAD_DIM
MAX_ROW = len(Q_PARTS) * TERM_ROWS
ROWS = MAX_ROW + 4

PHASES = ((0, 0), (0, 1), (1, 0), (0, 2), (1, 1), (0, 3), (1, 2), (1, 3))
TURNS = 2
PHASE_SLOTS = GROUPS * BLOCKS
SLOTS = len(PHASES) * PHASE_SLOTS
LOOP, LOOP_END, AFTER = (PHASE_SLOTS * p for p in (2, 4, 6))
LEAD = 6

UNITS = {
    0: (((0, (0, 2, 1, 3)), (1, (0, 1)), (1, (2, 3))), ((2, (0,)), (2, (1,)), (2, (2,))),
        ((2, (3,)), (3, (0,)), (3, (1,))), ((3, (2,)), (3, (3,)))),
    1: tuple(tuple((qb, (j,)) for j in range(GROUP)) for qb in range(BLOCKS)),
}
ONE_EACH = tuple((j,) for j in range(GROUP))
TILES = {
    0: (ONE_EACH, ONE_EACH, ((0, 1), (2, 3)), ((0, 1, 2, 3),)),
    1: (ONE_EACH,) * BLOCKS,
}
SCORE_BANKS, MAX_BANKS = 3, 3


def layer_of(slot):
    return PHASES[slot // PHASE_SLOTS][0]


def stack_of(slot):
    return slot // PHASE_SLOTS % 2


def units_of(slot):
    return UNITS[layer_of(slot)][slot % BLOCKS]


def tiles_of(slot):
    return TILES[layer_of(slot)][slot % BLOCKS]


UNITS_BEFORE = [0]
TILES_BEFORE = [0]
for _s in range(SLOTS):
    UNITS_BEFORE.append(UNITS_BEFORE[-1] + len(units_of(_s)))
    TILES_BEFORE.append(TILES_BEFORE[-1] + len(tiles_of(_s)))
T_SLOTS = LOOP_END - LOOP
T_GROUPS = T_SLOTS // BLOCKS
T_UNITS = UNITS_BEFORE[LOOP_END] - UNITS_BEFORE[LOOP]
T_TILES = TILES_BEFORE[LOOP_END] - TILES_BEFORE[LOOP]
ALL_GROUPS = SLOTS // BLOCKS
P_RING = 2

USES_MISC = {"q": ("turn", "q", "k", "v"), "m": ("turn", "linear", "turn2", "q", "k", "v"),
             "e": ("turn", "out", "turn2", "fc0", "fc1", "fc2", "fc3", "proj", "network", "count"),
             "w": ("weights_turned", "weights_1", "weights_2", "weights_3", "circulants", "bias_columns",
                   "low_rank", "fc_turned", "proj_turned")}
E_LAST = ("turn", "out", "scale2", "turn2", "network", "decay2", "spike1", "fire2", "decay3", "spike2", "fire3",
          "decay4", "spike3", "fire4", "decay5", "spike4", "fire5", "spike5", "count")
LOADS = [("q", 0), ("q", 1), ("m", 0), ("q", 2), ("m", 1), ("q", 3), ("m", 2), ("m", 3)]

W_STEPS = {"bias_order": 2.5, "circulants": 4.5, "bias_columns": 6.5, "int4": 5.5, "low_rank": 7.0, "fc_turned": 9.0,
           "proj_turned": 11.0}
Q_FIRST = {"norm": 1.5, "scale": 2.5, "turn": 3.5, "q": 4.0, "k": 4.5, "v": 6.0}
Q_LOOP = {"norm": 1.5, "scale": 2.5, "turn": 3.5, "q": 4, "k": 5.5, "v": 8.5}
M_SHORT = {"add": 1.5, "norm": 1.5, "scale": 2.5, "turn": 2.5, "linear": 3, "scale2": 4, "turn2": 4.5, "keep": 6.0,
           "q": 5.0, "k": 6.0, "v": 8.0}
M_LOOP = {"add": 1.5, "norm": 8.5, "scale": 9.5, "turn": 10.5, "linear": 12.5, "scale2": 13.5, "turn2": 14.5,
          "q": 15.0, "k": 15.5}
M_REST = {"v": 0.5, "keep": 4.0}
E_LOOP = {"turn": 1.5, "out": 2.5, "scale2": 3.5, "turn2": 4.5, "fc0": 4.5, "fc1": 5.5, "fc2": 6.5, "fc3": 7,
          "proj_half": 7.5, "proj": 8, "decay2": 8.5, "spike1": 8.5, "fire2": 9.5, "decay3": 9.5, "spike2": 9.5,
          "fire3": 11.5, "decay4": 11.5, "spike3": 11.5, "fire4": 13.0, "decay5": 13.0, "spike4": 13.0, "fire5": 14.0,
          "spike5": 15.5, "count": 15.5}


def side_steps():
    at = {s: ([], []) for s in range(SLOTS)}

    def place(chain, batch, phase, steps):
        for name, s in steps.items():
            at[phase * PHASE_SLOTS + int(s)][s != int(s)].append((chain, name, batch))

    place("q", 1, 0, Q_FIRST)
    place("w", 0, 0, W_STEPS)
    place("m", 0, 1, M_SHORT)
    for k in range(TURNS):
        place("q", k + 2, 2 * k + 2, Q_LOOP)
        place("m", k + 1, 2 * k + 2, M_LOOP)
        place("m", k + 1, 2 * k + 3, {"v": M_REST["v"]})
        place("e", k, 2 * k + 3, E_LOOP)
        place("m", k + 1, 2 * k + 3, {"keep": M_REST["keep"]})
    place("m", 3, 6, {k: v for k, v in M_SHORT.items() if k != "keep"})
    place("e", 2, 7, E_LOOP)
    place("m", 3, 7, {"keep": M_REST["keep"]})
    return at


SIDE_STEPS = side_steps()


def early_misc(slot):
    group, at = divmod(slot, BLOCKS)
    if at == 1 and group > 0:
        return [("heads", group - 1)]
    if at == 2 and group + 1 < ALL_GROUPS:
        return [("max", group + 1)]
    return []


def side_misc(steps):
    return [(c + "." + s, n) for c, s, n in steps if s in USES_MISC[c]]


START = [("q", "norm", 0), ("w", "weights_turned", 0), ("w", "weights_1", 0), ("w", "weights_2", 0),
         ("w", "weights_3", 0), ("q", "scale", 0), ("q", "turn", 0), ("q", "q", 0), ("q", "k", 0), ("q", "v", 0)]
MISC_ORDER = side_misc(START) + [("max", 0)]
MISC_SLOT = []
for _s in range(SLOTS):
    MISC_SLOT.append(len(MISC_ORDER))
    MISC_ORDER += early_misc(_s) + side_misc(SIDE_STEPS[_s][0]) + side_misc(SIDE_STEPS[_s][1])
T_MISC = MISC_SLOT[LOOP_END] - MISC_SLOT[LOOP]
MISC_ORDER += [("heads", ALL_GROUPS - 1)] + side_misc([("e", s, BATCHES - 1) for s in E_LAST])
MISC_AT = {u: k for k, u in enumerate(MISC_ORDER)}

STACK_DMAS = len(Q_PARTS) + 2 * len(K_PARTS) + 1
STACK_DONE = 16 * STACK_DMAS


def loads_of(chain, batch):
    return [(chain, batch, "zero", 0, 0, 0)] + [
        (chain, batch, t, part, term, half)
        for t, of in (("q", Q_PARTS), ("k", K_PARTS)) for part in range(3)
        for term in range(len(of)) if of[term] == part for half in range(1 if t == "q" else 2)]


def load_steps():
    at = {s: [] for s in range(SLOTS)}
    for (chain, batch), phase, first, each in (
            (("q", 1), 0, 5, 5), (("m", 0), 1, 5, 5), (("q", 2), 2, 4, 5),
            (("m", 1), 3, 0, 3), (("q", 3), 4, 4, 5), (("m", 2), 5, 0, 3), (("m", 3), 6, 5, 5)):
        for k, load in enumerate(loads_of(chain, batch)):
            at[phase * PHASE_SLOTS + first + k // each].append(load)
    return at


LOAD_STEPS = load_steps()


def build_program(nc, x_in, w_dq, w_uq, w_dkv, w_uk, w_uv, w_o, ffn_w, ffn_bias, ffn_a, ffn_b,
                  wq_c, wq_b, wk_c, wk_b, wv_c, wv_b, wo_c, wo_b, w_fc, w_proj, out):
    with ExitStack() as ctx:
        def sb(name, shape, dt=F32):
            return ctx.enter_context(nc.sbuf_tensor(name, shape, dt))

        def sem(name):
            return ctx.enter_context(nc.semaphore(name))

        score_banks = [ctx.enter_context(nc.psum_tensor(f"score_bank{k}", [P, 512], F32)) for k in range(SCORE_BANKS)]
        max_banks = [ctx.enter_context(nc.psum_tensor(f"max_bank{k}", [P, 512], F32)) for k in range(MAX_BANKS)]
        fc_banks = score_banks + max_banks[:CHUNKS - SCORE_BANKS]
        heads_bank = ctx.enter_context(nc.psum_tensor("heads_bank", [P, TOKENS], F32))
        misc = ctx.enter_context(nc.psum_tensor("misc", [P, 512], F32))

        ident = sb("ident", [P, P])
        ident_bf = sb("ident_bf", [P, P], BF16)
        flip = sb("flip", [P, P])
        mask_qk = sb("mask_qk", [P, P], BF16)
        mask_kq = sb("mask_kq", [P, P], BF16)
        minus_ones = sb("minus_ones", [2, TOKENS], BF16)
        zero_rows = sb("zero_rows", [4, TOKENS], BF16)
        minus_half = sb("minus_half", [P, BLOCKS])
        one = sb("one", [1, 1])

        raw_dq, raw_dkv = sb("raw_dq", [LATENT, P]), sb("raw_dkv", [LATENT, P])
        raw_uq, raw_uk, raw_uv = sb("raw_uq", [P, LATENT]), sb("raw_uk", [P, LATENT]), sb("raw_uv", [P, LATENT])
        raw_o, raw_int4 = sb("raw_o", [P, P]), sb("raw_int4", [P, P])
        raw_a, raw_b = sb("raw_a", [P, RANK]), sb("raw_b", [RANK, P])
        raw_fc, raw_proj = sb("raw_fc", [P, CHUNKS, P]), sb("raw_proj", [P, FEATURES])
        hankel = sb("hankel", [P, 4, P])
        bias_rows = sb("bias_rows", [1, 2, P])
        bias_ordered = sb("bias_ordered", [1, 2, P])
        uq_t, o_t, a_t = sb("uq_t", [LATENT, P]), sb("o_t", [P, P]), sb("a_t", [RANK, P])
        qk_t, v_eff, k_eff_t = sb("qk_t", [P, P]), sb("v_eff", [LATENT, P]), sb("k_eff_t", [LATENT, P])
        wq = [sb(f"wq{l}", [P, P]) for l in range(2)]
        wk = [sb(f"wk{l}", [P, P]) for l in range(2)]
        wv = [sb(f"wv{l}", [P, P]) for l in range(2)]
        w_linear, w_out = sb("w_linear", [P, P]), sb("w_out", [P, P])
        fc_t, proj_t = sb("fc_t", [P, FEATURES]), sb("proj_t", [P, CHUNKS, P])
        bias_q, bias_k = sb("bias_q", [P, 1]), sb("bias_k", [P, 1])
        linear_bias, v_bias, out_bias = (sb(n, [P, P]) for n in ("linear_bias", "v_bias", "out_bias"))
        absmax, scale4, inv4 = sb("absmax", [P, 1]), sb("scale4", [P, 2]), sb("inv4", [P, 1])
        int4 = sb("int4", [P, P])

        q_stack = [sb(f"q_stack{n}", [P, PAIRS, TOKENS], BF16) for n in range(2)]
        k_stack = [sb(f"k_stack{n}", [P, PAIRS, 2, TOKENS], BF16) for n in range(2)]
        v_ones = [sb(f"v_ones{n}", [P, BLOCKS, HEADS, HEAD_DIM + 1]) for n in range(2)]
        heads = [sb(f"heads{n}", [P, BLOCKS, P]) for n in range(2)]
        probs = [sb(f"probs{k}", [P, GROUP * TOKENS]) for k in range(P_RING)]
        row_max = [sb(f"row_max{k}", [P, 2 * 2 * BLOCKS]) for k in range(2)]
        max_parts = [sb(f"max_parts{k}", [P, 2, 2 * 2 * BLOCKS], BF16) for k in range(2)]
        max_rows = [sb(f"max_rows{k}", [32, P], BF16) for k in range(2)]
        heads_t = [sb(f"heads_t{k}", [P, TOKENS]) for k in range(2)]
        inv_sum = sb("inv_sum", [P, BLOCKS, GROUP])

        x_normed, x_added = sb("x_normed", [P, BLOCKS, P]), sb("x_added", [P, BLOCKS, P])
        x1, x1_biased, x2, x2_biased, x3 = (sb(n, [P, BLOCKS, P]) for n in ("x1", "x1_biased", "x2", "x2_biased", "x3"))
        NORMS = ("q", "m", "m2", "e")
        stats = {k: sb("stats_" + k, [P, BLOCKS, 6]) for k in NORMS}
        mean_var = {k: sb("mean_var_" + k, [P, BLOCKS, 2]) for k in NORMS}
        var_eps = {k: sb("var_eps_" + k, [P, BLOCKS]) for k in NORMS}
        rstd = {k: sb("rstd_" + k, [P, BLOCKS]) for k in NORMS}
        normed = {k: sb("normed_" + k, [P, BLOCKS, P]) for k in NORMS}
        normed_t = {k: sb("normed_t_" + k, [P, TOKENS]) for k in NORMS}
        full = {t: sb(f"full_{t}", [P, TOKENS]) for t in "qk"}
        rest = sb("rest", [P, TOKENS])
        parts = {t: sb(f"parts_{t}", [P, 3, TOKENS], BF16) for t in "qk"}
        heads_all_t = sb("heads_all_t", [P, TOKENS])
        relu = sb("relu", [P, TOKENS])
        hidden = sb("hidden", [P, CHUNKS, TOKENS])
        drive, decayed = sb("drive", [P, TOKENS]), sb("decayed", [P, TOKENS])
        membranes = [sb(f"membrane{k}", [P, TOKENS]) for k in range(2)]
        spikes = sb("spikes", [P, STEPS, TOKENS], BF16)
        result = sb("result", [P, BLOCKS, P])

        x_normed_loaded, x_added_loaded = sem("x_normed_loaded"), sem("x_added_loaded")
        w_loaded = [sem(f"w_loaded{k}") for k in range(3)]
        w1_loaded, doubled = sem("w1_loaded"), sem("doubled")
        consts_ready, pool_step = sem("consts_ready"), sem("pool_step")
        stacks_zeroed, stack1_zeroed, v_prepared = sem("stacks_zeroed"), sem("stack1_zeroed"), sem("v_prepared")
        minus_loaded = [sem(f"minus_loaded{n}") for n in range(2)]
        absmax_ready, absmax_all, int4_step = sem("absmax_ready"), sem("absmax_all"), sem("int4_step")
        bias_ready = sem("bias_ready")
        misc_full, misc_free = sem("misc_full"), sem("misc_free")
        unit_full, unit_read = sem("unit_full"), sem("unit_read")
        max_high, max_split = sem("max_high"), sem("max_split")
        max_loaded = [sem(f"max_loaded{k}") for k in range(2)]
        tile_full, tile_read = sem("tile_full"), sem("tile_read")
        pv_done, heads_free = sem("pv_done"), sem("heads_free")
        inverted = sem("inverted")
        stack_loaded = [sem(f"stack_loaded{n}") for n in range(2)]
        stats_done = {k: sem("stats_done_" + k) for k in NORMS}
        mean_ready = {k: sem("mean_ready_" + k) for k in NORMS}
        eps_added = {k: sem("eps_added_" + k) for k in NORMS}
        rstd_ready = {k: sem("rstd_ready_" + k) for k in NORMS}
        normed_ready = {k: sem("normed_ready_" + k) for k in NORMS}
        rest_ready = {(l, t): sem(f"rest_ready_{t}{l}") for l in range(2) for t in "qk"}
        middle_ready = {(l, t): sem(f"middle_ready_{t}{l}") for l in range(2) for t in "qk"}
        low_ready = {(l, t): sem(f"low_ready_{t}{l}") for l in range(2) for t in "qk"}
        x1_ready, x1_biased_ready, x2_biased_ready = sem("x1_ready"), sem("x1_biased_ready"), sem("x2_biased_ready")
        fc_full, relu_odd_ready, hidden_odd_ready = sem("fc_full"), sem("relu_odd_ready"), sem("hidden_odd_ready")
        last_spike_ready = sem("last_spike_ready")
        relu_ready, hidden_ready = sem("relu_ready"), sem("hidden_ready")
        spike_ready, decay_ready = sem("spike_ready"), sem("decay_ready")
        membrane_ready, result_ready = sem("membrane_ready"), sem("result_ready")
        stored = sem("stored")
        waited = sem("waited")

        circ = nc.dram_tensor("circ_twice", (4, 2 * P), F32, kind="Internal")
        circ_ap = circ.ap()

        def misc_at(use, turn):
            return turn * T_MISC + MISC_AT[use]

        def last_spike(step, batch):
            return batch == BATCHES - 1 and step == f"spike{STEPS}"

        def drive_at(batch, turn):
            return misc_at(("e.network" if batch == BATCHES - 1 else "e.proj", batch), turn)

        def wait(eng, semaphore, value):
            if not isinstance(value, int) or value > 0:
                eng.wait_ge(semaphore, value)

        def wait_apart(eng, semaphore, value):
            eng.wait_ge(semaphore, value)
            eng.sem_inc(waited, 1)

        def q_blocks(l, kb):
            first = kb * P if l == 0 else 0
            return first, TOKENS - first

        def prob_view(k, l, kb, j):
            width = q_blocks(l, kb)[1]
            return probs[k][:, j * width:(j + 1) * width]

        def for_pairs(tile, rows):
            return tile[:].rearrange("p (o q) -> p o q", o=1).to_broadcast([rows, PAIRS, TOKENS])

        block = ctx.enter_context(nc.Block())

        @block.sync
        def _(sp):
            def load_x(x, batch, loaded):
                sp.dma_start(x[:], x_in[batch].rearrange("(b p) c -> p b c", p=P)).then_inc(loaded, 16)

            for loaded, weights in ((w_loaded[0], ((raw_uq, w_uq), (raw_o, w_o), (raw_a, ffn_a))),
                                    (w_loaded[1], ((raw_dq, w_dq), (raw_uv, w_uv)))):
                for dst, src in weights:
                    sp.dma_start(dst[:], src).then_inc(loaded, 16)
            load_x(x_normed, 0, x_normed_loaded)
            for dst, src in ((raw_dkv, w_dkv), (raw_uk, w_uk), (raw_b, ffn_b), (raw_int4, ffn_w)):
                sp.dma_start(dst[:], src).then_inc(w_loaded[2], 16)
            def load_minus_ones(n):
                for half in range(2):
                    rows = k_stack[n][MAX_ROW + half:ROWS:2, :, half, :]
                    sp.dma_start(rows, for_pairs(minus_ones, 2)).then_inc(minus_loaded[n], 16)

            sp.wait_ge(stacks_zeroed, 3)
            load_minus_ones(0)
            sp.sem_inc(stored, 16)

            def load_stack(chain, batch, t, part, term, half, turn):
                number = LOADS.index((chain, batch))
                n, l = number % 2, 0 if chain == "q" else 1
                if t == "zero":
                    if number > 1:
                        sp.wait_ge(tile_full, turn * T_TILES + TILES_BEFORE[(number - 1) * PHASE_SLOTS])
                    sp.dma_start(q_stack[n][MAX_ROW:ROWS, :, :], for_pairs(zero_rows, 4)).then_inc(stack_loaded[n], 16)
                    return
                if part == 0:
                    sp.wait_ge(misc_free, misc_at((chain + "." + t, batch), turn) + 1)
                else:
                    sp.wait_ge((middle_ready, low_ready)[part - 1][(l, t)], turn + batch + 1)
                first = term * TERM_ROWS
                if t == "q":
                    to, src = q_stack[n][first:first + TERM_ROWS, :, :], parts[t][:, part, :]
                else:
                    to = k_stack[n][first + half:first + TERM_ROWS:2, :, half, :]
                    src = parts[t][64 * half:64 * half + 64, part, :]
                sp.dma_start(to, src).then_inc(stack_loaded[n], 16)

            def store_result(batch, turn):
                sp.wait_ge(result_ready, turn + batch + 1)
                dst = out[turn + batch].rearrange("(b p) c -> p b c", p=P)
                sp.dma_start(dst, result[:]).then_inc(stored, 16)

            def load_max_rows(group, turn):
                n, g = group // GROUPS % 2, group % GROUPS
                sp.wait_ge(misc_free, misc_at(("max", group), turn) + 1)
                sp.dma_start(q_stack[n][MAX_ROW:ROWS, 2 * g:2 * g + 2, :].rearrange("p r (b q) -> p (r b) q", b=BLOCKS),
                             max_rows[group % 2][:]).then_inc(max_loaded[group % 2], 16)

            for load in loads_of("q", 0):
                load_stack(*load, 0)
            load_x(x_normed, 1, x_normed_loaded)
            load_x(x_added, 0, x_added_loaded)
            sp.wait_ge(stack1_zeroed, 1)
            load_minus_ones(1)
            load_max_rows(0, 0)

            def slot(s, turn):
                if s == LOOP or s == AFTER:
                    batch = 1 if s == LOOP else 3
                    sp.wait_ge(x1_ready, turn + batch)
                    load_x(x_added, turn + batch, x_added_loaded)
                if s == LOOP:
                    sp.wait_ge(normed_ready["q"], turn + 2)
                    load_x(x_normed, turn + 2, x_normed_loaded)
                for kind, group in early_misc(s):
                    if kind == "max":
                        load_max_rows(group, turn)
                for load in LOAD_STEPS[s]:
                    load_stack(*load, turn)
                for chain, step, batch in SIDE_STEPS[s][0] + SIDE_STEPS[s][1]:
                    if (chain, step) == ("e", "count"):
                        store_result(batch, turn)

            for s in range(LOOP):
                slot(s, 0)
            with sp.Fori(0, TURNS) as turn:
                for s in range(LOOP, LOOP_END):
                    slot(s, turn)
            for s in range(AFTER, SLOTS):
                slot(s, 0)
            store_result(BATCHES - 1, 0)
            sp.wait_ge(stored, 16 + 16 * BATCHES)

        @block.gpsimd
        def _(pool):
            steps = [0]

            def then_wait(ins):
                steps[0] += 1
                ins.then_inc(pool_step, 1)
                pool.wait_ge(pool_step, steps[0])

            pool.memset(ident[:], 0.0).then_inc(pool_step, 1)
            pool.memset(flip[:], 0.0).then_inc(pool_step, 1)
            pool.memset(mask_qk[:], 0.0).then_inc(pool_step, 1)
            pool.memset(mask_kq[:], 0.0).then_inc(pool_step, 1)
            pool.memset(minus_half[:], -0.5).then_inc(pool_step, 1)
            pool.memset(one[:], 1.0).then_inc(pool_step, 1)
            steps[0] = 6
            pool.wait_ge(pool_step, steps[0])
            then_wait(pool.affine_select(out=ident[:], in_=ident[:], pattern=[[-1, P]], compare_op=ALU.not_equal,
                                         fill=1.0, base=0, channel_multiplier=1))
            then_wait(pool.tensor_copy(ident_bf[:], ident[:]))
            then_wait(pool.affine_select(out=flip[:], in_=flip[:], pattern=[[1, P]], compare_op=ALU.not_equal,
                                         fill=1.0, base=-P, channel_multiplier=1))
            then_wait(pool.affine_select(out=flip[:], in_=flip[:], pattern=[[1, P]], compare_op=ALU.not_equal,
                                         fill=1.0, base=0, channel_multiplier=1))
            pool.affine_select(out=mask_qk[:], in_=mask_qk[:], pattern=[[-1, P]], compare_op=ALU.is_ge,
                               fill=MASKED, base=0, channel_multiplier=1).then_inc(consts_ready, 1)
            pool.affine_select(out=mask_kq[:], in_=mask_kq[:], pattern=[[1, P]], compare_op=ALU.is_ge,
                               fill=MASKED, base=0, channel_multiplier=-1).then_inc(consts_ready, 1)

            def inverse_std(k, run):
                wait_apart(pool, mean_ready[k], run + 1)
                pool.tensor_scalar(var_eps[k][:], mean_var[k][:, :, 1], 1.0, LN_EPS, ALU.mult, ALU.add
                                   ).then_inc(eps_added[k], 1)
                pool.wait_ge(eps_added[k], run + 1)
                pool.tensor_tensor(rstd[k][:], var_eps[k][:], minus_half[:], ALU.pow).then_inc(rstd_ready[k], 1)

            def split(l, t, use, run):
                key = (l, t)
                pool.wait_ge(misc_free, use + 1)
                pool.tensor_tensor(rest[:], full[t][:], parts[t][:, 0, :], ALU.subtract
                                   ).then_inc(rest_ready[key], 1)
                wait_apart(pool, rest_ready[key], run + 1)
                pool.tensor_scalar(parts[t][:, 1, :], rest[:], 1.0, 0.0, ALU.mult, ALU.add
                                   ).then_inc(middle_ready[key], 1)
                pool.wait_ge(middle_ready[key], run + 1)
                pool.tensor_tensor(parts[t][:, 2, :], rest[:], parts[t][:, 1, :], ALU.subtract
                                   ).then_inc(low_ready[key], 1)
                pool.wait_ge(low_ready[key], run + 1)

            def rows_of(tile):
                return tile[:].rearrange("p (o c) -> p o c", o=1).to_broadcast([P, BLOCKS, P])

            def side(chain, step, n, turn):
                run = turn + n
                if chain in ("q", "m") and step in ("q", "k"):
                    split(0 if chain == "q" else 1, step, misc_at((chain + "." + step, n), turn), run)
                elif (chain, step) in (("q", "norm"), ("m", "norm")):
                    inverse_std(chain, run)
                elif (chain, step) == ("m", "add"):
                    phase = PHASES.index((0, n))
                    pool.wait_ge(misc_free, misc_at(("heads", GROUPS * (phase + 1) - 1), turn) + 1)
                    pool.wait_ge(x_added_loaded, turn * 16 + 16 * (n + 1))
                    pool.tensor_tensor(x1[:], x_added[:], heads[phase % 2][:], ALU.add).then_inc(x1_ready, 1)
                    pool.wait_ge(x1_ready, run + 1)
                    pool.tensor_tensor(x1_biased[:], x1[:], rows_of(linear_bias), ALU.add).then_inc(x1_biased_ready, 1)
                elif (chain, step) == ("m", "linear"):
                    inverse_std("m2", run)
                elif (chain, step) == ("m", "keep"):
                    if n > 0:
                        pool.wait_ge(misc_free, misc_at(("e.out", n - 1), turn) + 1)
                    pool.tensor_tensor(x2_biased[:], x2[:], rows_of(out_bias), ALU.add).then_inc(x2_biased_ready, 1)
                elif (chain, step) == ("e", "out"):
                    inverse_std("e", run)
                elif chain == "e" and step.startswith("spike") and not last_spike(step, n):
                    k = int(step[-1])
                    if k == 1:
                        wait_apart(pool, misc_free, drive_at(n, turn) + 1)
                        pool.tensor_scalar(spikes[:, 0, :], drive[:], THRESHOLD, None, ALU.is_gt).then_inc(spike_ready, 1)
                    else:
                        wait_apart(pool, membrane_ready, turn * (STEPS - 1) + n * (STEPS - 1) + k - 1)
                        pool.tensor_scalar(spikes[:, k - 1, :], membranes[k % 2][:], -THRESHOLD, None, ALU.is_lt
                                           ).then_inc(spike_ready, 1)
                elif (chain, step) == ("w", "bias_order"):
                    pool.wait_ge(w1_loaded, 16 * 11)
                    for k, (a, b, order) in enumerate(((HEAD_DIM, 2, "o (r a d) -> o d a r"),
                                                       (2, HEAD_DIM, "o (r a d) -> o a d r"))):
                        pool.tensor_copy(bias_ordered[:, k, :].rearrange("o (x y r) -> o x y r", x=a, y=b),
                                         bias_rows[:, k, :].rearrange(order, a=2, d=HEAD_DIM)).then_inc(bias_ready, 1)

            for step in START:
                side(*step, 0)
            pool.memset(k_stack[1][:].rearrange("p r a q -> p (r a q)").bitcast(F32), 0.0).then_inc(stack1_zeroed, 1)
            for w, c in enumerate((wq_c, wk_c, wv_c, wo_c)):
                twice = circ_ap[w:w + 1, :].rearrange("o (r n) -> o r n", r=2)
                for r in range(2):
                    pool.dma_start(twice[:, r, :], c.rearrange("(o n) -> o n", o=1)).then_inc(doubled, 16)
            for k, b in enumerate((wq_b, wk_b)):
                pool.dma_start(bias_rows[:, k, :], b.rearrange("(o n) -> o n", o=1)).then_inc(w1_loaded, 16)
            for dst, src in ((linear_bias, ffn_bias), (v_bias, wv_b), (out_bias, wo_b)):
                pool.dma_start(dst[:], src.rearrange("(o n) -> o n", o=1).to_broadcast([P, P])).then_inc(w1_loaded, 16)
            pool.dma_start(raw_fc[:], w_fc.rearrange("(f p) c -> p f c", p=P)).then_inc(w1_loaded, 16)
            pool.dma_start(raw_proj[:], w_proj).then_inc(w1_loaded, 16)
            pool.wait_ge(doubled, 16 * 8)
            for w in range(4):
                window = bass.AP(tensor=circ_ap.tensor, offset=w * 2 * P, ap=[[1, P], [1, P]])
                pool.dma_start(hankel[:, w, :], window).then_inc(w1_loaded, 16)
            pool.wait_ge(absmax_ready, 1)
            pool.partition_all_reduce(scale4[:, 0:1], absmax[:], P, bass.bass_isa.ReduceOp.max).then_inc(absmax_all, 1)

            def slot(s, turn):
                for step in SIDE_STEPS[s][0]:
                    side(*step, turn)
                for step in SIDE_STEPS[s][1]:
                    side(*step, turn)

            for s in range(LOOP):
                slot(s, 0)
            with pool.Fori(0, TURNS) as turn:
                for s in range(LOOP, LOOP_END):
                    slot(s, turn)
            for s in range(AFTER, SLOTS):
                slot(s, 0)
            for step in E_LAST:
                side("e", step, BATCHES - 1, 0)

        @block.tensor
        def _(pe):
            def open_misc(use):
                wait(pe, misc_free, use)

            def turn_blocks(src):
                for b in range(BLOCKS):
                    last = pe.transpose(misc[:, b * P:(b + 1) * P], src[:, b, :], ident[:])
                last.then_inc(misc_full, 1)

            def by_token(src_t, w):
                for b in range(BLOCKS):
                    last = pe.matmul(misc[:, b * P:(b + 1) * P], src_t[:, b * P:(b + 1) * P], w[:], start=True, stop=True)
                last.then_inc(misc_full, 1)

            def project(n, turn, first):
                half = CHUNKS // 2
                chunks = range(half) if first else range(half, CHUNKS)
                if first:
                    open_misc(drive_at(n, turn))
                pe.wait_ge(hidden_ready, turn * CHUNKS + n * CHUNKS + chunks[-1] + 1)
                for f in chunks:
                    last = pe.matmul(misc[:], proj_t[:, f, :], hidden[:, f, :], start=(f == 0), stop=(f == CHUNKS - 1))
                if not first:
                    last.then_inc(misc_full, 1)

            def side(chain, step, n, turn):
                if (chain, step) == ("e", "proj_half"):
                    project(n, turn, first=True)
                if step not in USES_MISC[chain]:
                    return
                if chain == "w":
                    setup(step)
                    return
                if step == "proj":
                    project(n, turn, first=False)
                    return
                run = turn + n
                l = 0 if chain == "q" else 1
                k2 = {"q": "q", "m": "m2"}.get(chain)
                open_misc(misc_at((chain + "." + step, n), turn))
                if step == "turn" and chain != "e":
                    pe.wait_ge(normed_ready[chain], run + 1)
                    turn_blocks(normed[chain])
                elif step == "turn":
                    turn_blocks(heads[PHASES.index((1, n)) % 2])
                elif step == "turn2":
                    k = "m2" if chain == "m" else "e"
                    pe.wait_ge(normed_ready[k], run + 1)
                    turn_blocks(normed[k])
                elif step in ("q", "k"):
                    w = (wq if step == "q" else wk)[l]
                    pe.matmul(misc[:], w[:], normed_t[k2][:], start=True, stop=True).then_inc(misc_full, 1)
                elif step == "v":
                    by_token(normed_t[k2], wv[l])
                elif step == "linear":
                    by_token(normed_t["m"], w_linear)
                elif step == "out":
                    by_token(heads_all_t, w_out)
                elif step.startswith("fc"):
                    f = int(step[2:])
                    pe.matmul(misc[:], fc_t[:, f * P:(f + 1) * P], normed_t["e"][:], start=True, stop=True
                              ).then_inc(misc_full, 1)
                elif step == "network":
                    pe.wait_ge(tile_read, TILES_BEFORE[SLOTS] + SCORE_BANKS)
                    pe.wait_ge(unit_read, UNITS_BEFORE[SLOTS])
                    for f in range(CHUNKS):
                        pe.matmul(fc_banks[f][:], fc_t[:, f * P:(f + 1) * P], normed_t["e"][:], start=True, stop=True
                                  ).then_inc(fc_full, 1)
                    for f in range(CHUNKS):
                        if f % 2 == 0:
                            pe.wait_ge(hidden_ready, CHUNKS * n + f // 2 + 1)
                        else:
                            pe.wait_ge(hidden_odd_ready, f // 2 + 1)
                        last = pe.matmul(misc[:], proj_t[:, f, :], hidden[:, f, :], start=(f == 0), stop=(f == CHUNKS - 1))
                    last.then_inc(misc_full, 1)
                elif step == "count":
                    last_batch = n == BATCHES - 1
                    for k in range(STEPS):
                        if last_batch and k == STEPS - 1:
                            pe.wait_ge(last_spike_ready, 1)
                        elif last_batch:
                            pe.wait_ge(spike_ready, n * STEPS + k + 1)
                        elif k == 0:
                            pe.wait_ge(spike_ready, turn * STEPS + n * STEPS + STEPS)
                        for b in range(BLOCKS):
                            last = pe.matmul(misc[:, b * P:(b + 1) * P], spikes[:, k, b * P:(b + 1) * P], ident_bf[:],
                                             start=(k == 0 and b == 0), stop=(k == STEPS - 1), skip_group_check=True)
                    last.then_inc(misc_full, 1)

            def score_unit(slot, u, turn):
                l, n = layer_of(slot), stack_of(slot)
                g = slot // BLOCKS % GROUPS
                qb, js = units_of(slot)[u]
                count = turn * T_UNITS + UNITS_BEFORE[slot] + u
                bank = max_banks[(UNITS_BEFORE[slot] + u) % MAX_BANKS]
                if slot % PHASE_SLOTS == 0 and u == 0:
                    if slot == PHASE_SLOTS:
                        pe.wait_ge(minus_loaded[1], 16 * 2)
                    pe.wait_ge(stack_loaded[n], turn * STACK_DONE + (slot // (2 * PHASE_SLOTS) + 1) * STACK_DONE)
                wait(pe, unit_read, count - MAX_BANKS + 1)
                width = (qb + 1) * P if l == 0 else TOKENS
                for k, j in enumerate(js):
                    pair, half = 2 * g + j // 2, j % 2
                    last = pe.matmul(bank[:, k * width:(k + 1) * width], q_stack[n][0:ROWS, pair, qb * P:(qb + 1) * P],
                                     k_stack[n][0:ROWS, pair, half, 0:width], start=True, stop=(l == 1))
                    if l == 0:
                        last = pe.matmul(bank[:, (k + 1) * width - P:(k + 1) * width], ident_bf[:], mask_qk[:],
                                         start=False, stop=True)
                last.then_inc(unit_full, 1)

            def turn_max(group, turn):
                use = misc_at(("max", group), turn)
                open_misc(use)
                pe.wait_ge(max_split, turn * T_GROUPS + group + 1)
                pe.transpose(misc[0:32, 0:P // 2].bitcast(BF16), max_parts[group % 2][:].rearrange("p a c -> p (a c)"),
                             ident_bf[:]).then_inc(misc_full, 1)

            def turn_heads(group, turn):
                use = misc_at(("heads", group), turn)
                open_misc(use)
                pe.wait_ge(heads_free, turn * T_GROUPS + group + 2)
                for b in range(BLOCKS):
                    last = pe.transpose(misc[:, b * P:(b + 1) * P], heads_t[group % 2][:, b * P:(b + 1) * P], ident[:])
                last.then_inc(misc_full, 1)

            def score_tile(slot, t, turn):
                l, n = layer_of(slot), stack_of(slot)
                group, kb = divmod(slot, BLOCKS)
                g = group % GROUPS
                index = TILES_BEFORE[slot] + t
                bank = score_banks[index % SCORE_BANKS]
                if kb == 0 and t == 0:
                    pe.wait_ge(max_loaded[group % 2], turn * (16 * T_GROUPS // 2) + 16 * (group // 2 + 1))
                pe.wait_ge(tile_read, turn * T_TILES + index + 1)
                first, width = q_blocks(l, kb)
                for k, j in enumerate(tiles_of(slot)[t]):
                    pair, half = 2 * g + j // 2, j % 2
                    at = bank[:, k * width:(k + 1) * width]
                    last = pe.matmul(at, k_stack[n][0:ROWS, pair, half, kb * P:(kb + 1) * P],
                                     q_stack[n][0:ROWS, pair, first:TOKENS], start=True, stop=(l == 1))
                    if l == 0:
                        last = pe.matmul(at[:, 0:P], ident_bf[:], mask_kq[:], start=False, stop=True)
                last.then_inc(tile_full, 1)

            def times_v(slot, js, turn):
                l, n = layer_of(slot), stack_of(slot)
                group, kb = divmod(slot, BLOCKS)
                first, width = q_blocks(l, kb)
                if js[0] == 0:
                    pe.wait_ge(tile_read, turn * T_TILES + TILES_BEFORE[slot + 1] + SCORE_BANKS)
                    if kb == 0:
                        pe.wait_ge(heads_free, turn * T_GROUPS + group + 1)
                for j in js:
                    h = GROUP * (group % GROUPS) + j
                    last = pe.matmul(heads_bank[32 * j:32 * j + HEAD_DIM + 1, first:TOKENS], v_ones[n][:, kb, h, :],
                                     prob_view(slot % P_RING, l, kb, j), start=(kb == 0), stop=(kb == BLOCKS - 1),
                                     skip_group_check=True, tile_position=(0, 32 * j))
                if js[-1] == GROUP - 1:
                    last.then_inc(pv_done, 1)

            def setup(name):
                open_misc(misc_at(("w." + name, 0), 0))
                if name == "weights_turned":
                    pe.wait_ge(consts_ready, 2)
                    pe.wait_ge(w_loaded[0], 16 * 3)
                    pe.transpose(misc[0:LATENT, 0:P], raw_uq[:], ident[:])
                    pe.transpose(misc[:, P:2 * P], raw_o[:], ident[:])
                    last = pe.transpose(misc[0:RANK, 2 * P:3 * P], raw_a[:], ident[:])
                elif name == "weights_1":
                    pe.wait_ge(w_loaded[1], 16 * 2)
                    pe.matmul(misc[:, 0:P], raw_dq[:], uq_t[:], start=True, stop=True)
                    pe.matmul(misc[:, P:2 * P], uq_t[:], raw_dq[:], start=True, stop=True)
                    last = pe.matmul(misc[0:LATENT, 2 * P:3 * P], raw_uv[:], o_t[:], start=True, stop=True)
                elif name == "weights_2":
                    pe.wait_ge(w_loaded[2], 16 * 4)
                    pe.matmul(misc[0:LATENT, 0:P], raw_uk[:], qk_t[:], start=True, stop=True)
                    last = pe.matmul(misc[:, P:2 * P], raw_dkv[:], v_eff[:], start=True, stop=True)
                elif name == "weights_3":
                    last = pe.matmul(misc[:, 0:P], raw_dkv[:], k_eff_t[:], start=True, stop=True)
                elif name == "circulants":
                    pe.wait_ge(w1_loaded, 16 * 11)
                    for w in range(4):
                        last = pe.matmul(misc[:, w * P:(w + 1) * P], flip[:], hankel[:, w, :], start=True, stop=True)
                elif name == "low_rank":
                    last = pe.matmul(misc[:, 0:P], a_t[:], raw_b[:], start=True, stop=True)
                elif name == "bias_columns":
                    pe.wait_ge(bias_ready, 2)
                    for k in range(2):
                        last = pe.matmul(misc[:, k:k + 1], bias_ordered[:, k, :], one[:], start=True, stop=True)
                elif name == "fc_turned":
                    for f in range(CHUNKS):
                        last = pe.transpose(misc[:, f * P:(f + 1) * P], raw_fc[:, f, :], ident[:])
                elif name == "proj_turned":
                    for f in range(CHUNKS):
                        last = pe.transpose(misc[:, f * P:(f + 1) * P], raw_proj[:, f * P:(f + 1) * P], ident[:])
                last.then_inc(misc_full, 1)

            for step in START:
                side(*step, 0)
            pe.wait_ge(minus_loaded[0], 16 * 2)
            pe.wait_ge(v_prepared, 2)
            for s in range(LEAD):
                for u in range(len(units_of(s))):
                    score_unit(s, u, 0)
                if s == BLOCKS:
                    turn_max(0, 0)

            def slot(s, turn):
                units = list(range(len(units_of(s + LEAD)))) if s + LEAD < SLOTS else []
                tiles = list(range(len(tiles_of(s))))

                def scores(count):
                    for _ in range(count):
                        if tiles:
                            score_tile(s, tiles.pop(0), turn)
                        if units:
                            score_unit(s + LEAD, units.pop(0), turn)

                scores(2)
                for kind, group in early_misc(s):
                    (turn_max if kind == "max" else turn_heads)(group, turn)
                for step in SIDE_STEPS[s][0]:
                    side(*step, turn)
                if s > 0:
                    times_v(s - 1, (0, 1, 2, 3), turn)
                scores(2)
                for step in SIDE_STEPS[s][1]:
                    side(*step, turn)

            for s in range(LOOP):
                slot(s, 0)
            with pe.Fori(0, TURNS) as turn:
                for s in range(LOOP, LOOP_END):
                    slot(s, turn)
            for s in range(AFTER, SLOTS):
                slot(s, 0)
            times_v(SLOTS - 1, (0, 1, 2, 3), 0)
            turn_heads(ALL_GROUPS - 1, 0)
            for step in E_LAST:
                side("e", step, BATCHES - 1, 0)

        @block.vector
        def _(dve):
            def max_view(group):
                return row_max[group % 2][:].rearrange("p (a r b) -> p a r b", a=2, r=2)

            def reduce_unit(slot, u, turn):
                l, group = layer_of(slot), slot // BLOCKS
                qb, js = units_of(slot)[u]
                count = turn * T_UNITS + UNITS_BEFORE[slot] + u
                bank = max_banks[(UNITS_BEFORE[slot] + u) % MAX_BANKS]
                width = (qb + 1) * P if l == 0 else TOKENS
                to = max_view(group)
                scores = bank[:, 0:len(js) * width]
                if len(js) == 4:
                    to, scores = to[:, :, :, qb], scores.rearrange("p (a r q) -> p a r q", a=2, r=2)
                elif len(js) == 2:
                    to, scores = to[:, :, js[0] // 2, qb], scores.rearrange("p (a q) -> p a q", a=2)
                else:
                    to = to[:, js[0] % 2, js[0] // 2, qb:qb + 1]
                dve.wait_ge(unit_full, count + 1)
                dve.tensor_reduce(to, scores, AX_X, ALU.max).then_inc(unit_read, 1)

            def split_max(group, turn):
                dve.wait_ge(unit_read, turn * T_UNITS + UNITS_BEFORE[BLOCKS * (group + 1)])
                dve.tensor_copy(max_parts[group % 2][:, 0, :], row_max[group % 2][:]).then_inc(max_high, 1)
                dve.wait_ge(max_high, turn * T_GROUPS + group + 1)
                dve.tensor_tensor(max_parts[group % 2][:, 1, :], row_max[group % 2][:], max_parts[group % 2][:, 0, :],
                                  ALU.subtract).then_inc(max_split, 1)

            def divide_heads(group, turn):
                use = misc_at(("heads", group), turn)
                n, g = group // GROUPS % 2, group % GROUPS
                view = misc[:].rearrange("p (b j c) -> p b j c", b=BLOCKS, j=GROUP)
                dve.wait_ge(misc_full, use + 1)
                dve.reciprocal(inv_sum[:], view[:, :, :, HEAD_DIM]).then_inc(inverted, 1)
                dve.wait_ge(inverted, turn * T_GROUPS + group + 1)
                to = heads[n][:, :, g * 32:(g + 1) * 32].rearrange("p b (j d) -> p b j d", j=GROUP)
                inv = inv_sum[:].rearrange("p b (j o) -> p b j o", o=1).to_broadcast([P, BLOCKS, GROUP, HEAD_DIM])
                dve.tensor_tensor(to, view[:, :, :, 0:HEAD_DIM], inv, ALU.mult).then_inc(misc_free, 1)

            def statistics(k, x, run):
                for b in range(BLOCKS):
                    last = dve.bn_stats(stats[k][:, b, :], x[:, b, :])
                last.then_inc(stats_done[k], 1)
                wait_apart(dve, stats_done[k], run + 1)
                for b in range(BLOCKS):
                    last = dve.bn_aggr(mean_var[k][:, b, :], stats[k][:, b, :])
                last.then_inc(mean_ready[k], 1)

            def normalise(k, x, run):
                dve.wait_ge(rstd_ready[k], run + 1)
                for b in range(BLOCKS):
                    last = dve.tensor_scalar(normed[k][:, b, :], x[:, b, :], mean_var[k][:, b, 0:1], rstd[k][:, b:b + 1],
                                             ALU.subtract, ALU.mult)
                last.then_inc(normed_ready[k], 1)

            misc_blocks = misc[:].rearrange("p (b c) -> p b c", b=BLOCKS)

            def side(chain, step, n, turn):
                run = turn + n
                if (chain, step) == ("w", "int4"):
                    int4_weight()
                elif (chain, step) == ("w", "low_rank"):
                    dve.wait_ge(int4_step, 5)
                    dve.wait_ge(misc_full, misc_at(("w.low_rank", 0), 0) + 1)
                    dve.tensor_tensor(w_linear[:], misc[:, 0:P], int4[:], ALU.add).then_inc(misc_free, 1)
                elif (chain, step) == ("q", "norm"):
                    dve.wait_ge(x_normed_loaded, turn * 16 + 16 * (n + 1))
                    statistics("q", x_normed, run)
                elif (chain, step) == ("q", "scale"):
                    normalise("q", x_normed, run)
                elif (chain, step) == ("m", "norm"):
                    dve.wait_ge(x1_ready, run + 1)
                    statistics("m", x1, run)
                elif (chain, step) == ("m", "scale"):
                    normalise("m", x1, run)
                elif (chain, step) == ("m", "linear"):
                    dve.wait_ge(misc_full, misc_at(("m.linear", n), turn) + 1)
                    dve.wait_ge(x1_biased_ready, run + 1)
                    if n > 0:
                        dve.wait_ge(x2_biased_ready, turn + n)
                    dve.tensor_tensor(x2[:], misc_blocks, x1_biased[:], ALU.add).then_inc(misc_free, 1)
                    dve.wait_ge(misc_free, misc_at(("m.linear", n), turn) + 1)
                    statistics("m2", x2, run)
                elif (chain, step) == ("m", "scale2"):
                    normalise("m2", x2, run)
                elif (chain, step) == ("m", "v"):
                    dve.wait_ge(misc_full, misc_at(("m.v", n), turn) + 1)
                    to = v_ones[LOADS.index(("m", n)) % 2][:].rearrange("p b h c -> p (b h) c")[:, :, 0:HEAD_DIM]
                    dve.tensor_tensor(to, misc[:].rearrange("p (m d) -> p m d", d=HEAD_DIM),
                                      v_bias[:].rearrange("p (o c) -> p o c", o=1).to_broadcast([P, BLOCKS, P]),
                                      ALU.add).then_inc(misc_free, 1)
                elif (chain, step) == ("e", "out"):
                    dve.wait_ge(misc_full, misc_at(("e.out", n), turn) + 1)
                    dve.wait_ge(x2_biased_ready, run + 1)
                    dve.tensor_tensor(x3[:], misc_blocks, x2_biased[:], ALU.add).then_inc(misc_free, 1)
                    dve.wait_ge(misc_free, misc_at(("e.out", n), turn) + 1)
                    statistics("e", x3, run)
                elif (chain, step) == ("e", "scale2"):
                    normalise("e", x3, run)
                elif step == "network":
                    for k, f in enumerate(range(1, CHUNKS, 2)):
                        dve.wait_ge(fc_full, f + 1)
                        dve.tensor_scalar(membranes[k][:], fc_banks[f][:], 0.0, None, ALU.max).then_inc(relu_odd_ready, 1)
                        dve.wait_ge(relu_odd_ready, k + 1)
                        dve.tensor_tensor(hidden[:, f, :], membranes[k][:], membranes[k][:], ALU.mult
                                          ).then_inc(hidden_odd_ready, 1)
                elif chain == "e" and step[:-1] == "decay":
                    k = int(step[-1])
                    last, sign = (drive, 1.0) if k == 2 else (membranes[(k - 1) % 2], -1.0)
                    if k == 2:
                        dve.wait_ge(misc_free, drive_at(n, turn) + 1)
                    else:
                        dve.wait_ge(membrane_ready, turn * (STEPS - 1) + n * (STEPS - 1) + k - 2)
                    dve.scalar_tensor_tensor(out=decayed[:], in0=last[:], scalar=sign * DECAY, in1=drive[:],
                                             op0=ALU.mult, op1=ALU.add).then_inc(decay_ready, 1)
                elif chain == "e" and step[:-1] == "fire":
                    k = int(step[-1])
                    last, sign = (drive, 1.0) if k == 2 else (membranes[(k - 1) % 2], -1.0)
                    if k > 3:
                        dve.wait_ge(spike_ready, turn * STEPS + n * STEPS + k - 2)
                    dve.wait_ge(decay_ready, turn * (STEPS - 1) + n * (STEPS - 1) + k - 1)
                    dve.scalar_tensor_tensor(out=membranes[k % 2][:], in0=last[:], scalar=sign * THRESHOLD, in1=decayed[:],
                                             op0=ALU.is_gt if k == 2 else ALU.is_lt, op1=ALU.subtract
                                             ).then_inc(membrane_ready, 1)
                elif last_spike(step, n):
                    dve.wait_ge(membrane_ready, (STEPS - 1) * BATCHES)
                    dve.tensor_scalar(spikes[:, STEPS - 1, :], membranes[STEPS % 2][:], -THRESHOLD, None, ALU.is_lt
                                      ).then_inc(last_spike_ready, 1)
                elif (chain, step) == ("e", "count"):
                    dve.wait_ge(misc_full, misc_at(("e.count", n), turn) + 1)
                    dve.wait_ge(stored, turn * 16 + 16 * (n + 1))
                    dve.scalar_tensor_tensor(out=result[:].rearrange("p b c -> p (b c)"), in0=misc[:], scalar=1.0 / STEPS,
                                             in1=x3[:].rearrange("p b c -> p (b c)"), op0=ALU.mult, op1=ALU.add
                                             ).then_inc(misc_free, 1)
                    dve.wait_ge(misc_free, misc_at(("e.count", n), turn) + 1)
                    dve.sem_inc(result_ready, 1)

            def int4_weight():
                dve.wait_ge(absmax_all, 1)
                dve.tensor_scalar(scale4[:, 1:2], scale4[:, 0:1], 1.0 / INT4_MAX, None, ALU.mult).then_inc(int4_step, 1)
                dve.wait_ge(int4_step, 1)
                dve.reciprocal(inv4[:], scale4[:, 1:2]).then_inc(int4_step, 1)
                dve.wait_ge(int4_step, 2)
                dve.tensor_scalar(int4[:], raw_int4[:], inv4[:], ROUND, ALU.mult, ALU.add).then_inc(int4_step, 1)
                dve.wait_ge(int4_step, 3)
                dve.tensor_scalar(int4[:], int4[:], ROUND, -8.0, ALU.subtract, ALU.max).then_inc(int4_step, 1)
                dve.wait_ge(int4_step, 4)
                dve.tensor_scalar(int4[:], int4[:], 7.0, scale4[:, 1:2], ALU.min, ALU.mult).then_inc(int4_step, 1)

            dve.memset(minus_ones[:], -1.0).then_inc(stacks_zeroed, 1)
            dve.memset(zero_rows[:], 0.0).then_inc(stacks_zeroed, 1)
            dve.memset(k_stack[0][:].rearrange("p r a q -> p (r a q)").bitcast(F32), 0.0).then_inc(stacks_zeroed, 1)
            side("q", "norm", 0, 0)
            side("q", "scale", 0, 0)
            dve.memset(heads_bank[:], 0.0).then_inc(heads_free, 1)
            dve.wait_ge(w_loaded[2], 16 * 4)
            dve.tensor_reduce(absmax[:], raw_int4[:], AX_X, ALU.max, apply_absolute_value=True).then_inc(absmax_ready, 1)
            for n in range(2):
                dve.memset(v_ones[n][:, :, :, HEAD_DIM:HEAD_DIM + 1], 1.0).then_inc(v_prepared, 1)
            for s in range(LEAD):
                for u in range(len(units_of(s))):
                    reduce_unit(s, u, 0)
                if s == BLOCKS - 1:
                    split_max(0, 0)

            def slot(s, turn):
                ahead = s + LEAD
                todo = [u for u in range(len(units_of(ahead)))] if ahead < SLOTS else []
                for u in todo[:2]:
                    reduce_unit(ahead, u, turn)
                for kind, group in early_misc(s):
                    if kind == "heads":
                        divide_heads(group, turn)
                for step in SIDE_STEPS[s][0]:
                    side(*step, turn)
                for u in todo[2:]:
                    reduce_unit(ahead, u, turn)
                if ahead < SLOTS and ahead % BLOCKS == BLOCKS - 1:
                    split_max(ahead // BLOCKS, turn)
                for step in SIDE_STEPS[s][1]:
                    side(*step, turn)

            for s in range(LOOP):
                slot(s, 0)
            with dve.Fori(0, TURNS) as turn:
                for s in range(LOOP, LOOP_END):
                    slot(s, turn)
            for s in range(AFTER, SLOTS):
                slot(s, 0)
            divide_heads(ALL_GROUPS - 1, 0)
            for step in E_LAST:
                side("e", step, BATCHES - 1, 0)

        @block.scalar
        def _(act):
            def copy_out(to, use, src=None):
                act.wait_ge(misc_full, use + 1)
                act.copy(to, misc[:] if src is None else src).then_inc(misc_free, 1)

            def exp_tile(slot, t, turn):
                l, kb = layer_of(slot), slot % BLOCKS
                index = TILES_BEFORE[slot] + t
                js = tiles_of(slot)[t]
                width = q_blocks(l, kb)[1]
                src = score_banks[index % SCORE_BANKS][:, 0:len(js) * width]
                to = probs[slot % P_RING][:, js[0] * width:(js[-1] + 1) * width]
                act.wait_ge(tile_full, turn * T_TILES + index + 1)
                if t == 0:
                    act.wait_ge(pv_done, turn * T_SLOTS + slot + 1)
                act.activation(to, src, ACT.Exp).then_inc(tile_read, 1)

            def take_heads(group, turn):
                act.wait_ge(pv_done, turn * T_SLOTS + BLOCKS * (group + 1) + P_RING)
                act.copy(heads_t[group % 2][:], heads_bank[:]).then_inc(heads_free, 1)

            def take_max(group, turn):
                act.wait_ge(misc_full, misc_at(("max", group), turn) + 1)
                act.copy(max_rows[group % 2][:], misc[0:32, 0:P // 2].bitcast(BF16)).then_inc(misc_free, 1)

            def side(chain, step, n, turn):
                if step not in USES_MISC[chain]:
                    return
                if chain == "w":
                    setup(step)
                    return
                run = turn + n
                use = misc_at((chain + "." + step, n), turn)
                l = 0 if chain == "q" else 1
                if step == "turn":
                    copy_out({"q": normed_t["q"], "m": normed_t["m"], "e": heads_all_t}[chain][:], use)
                elif step == "turn2":
                    copy_out(normed_t["m2" if chain == "m" else "e"][:], use)
                elif step in ("q", "k"):
                    act.wait_ge(misc_full, use + 1)
                    number = LOADS.index((chain, n))
                    if number > 0:
                        act.wait_ge(stack_loaded[(number - 1) % 2], turn * STACK_DONE + ((number - 1) // 2 + 1) * STACK_DONE)
                    if l == 0:
                        act.copy(parts[step][:, 0, :], misc[:])
                        act.copy(full[step][:], misc[:]).then_inc(misc_free, 1)
                    else:
                        bias = {"q": bias_q, "k": bias_k}[step]
                        act.activation(parts[step][:, 0, :], misc[:], ACT.Identity, bias=bias[:])
                        act.activation(full[step][:], misc[:], ACT.Identity, bias=bias[:]).then_inc(misc_free, 1)
                elif (chain, step) == ("q", "v"):
                    act.wait_ge(misc_full, use + 1)
                    to = v_ones[LOADS.index(("q", n)) % 2][:].rearrange("p b h c -> p (b h) c")[:, :, 0:HEAD_DIM]
                    act.copy(to, misc[:].rearrange("p (m d) -> p m d", d=HEAD_DIM)).then_inc(misc_free, 1)
                elif step.startswith("fc"):
                    f = int(step[2:])
                    if n > 0 or f > 0:
                        act.wait_ge(hidden_ready, turn * CHUNKS + n * CHUNKS + f)
                    act.wait_ge(misc_full, use + 1)
                    act.activation(relu[:], misc[:], ACT.Relu).then_inc(misc_free, 1)
                    act.wait_ge(misc_free, use + 1)
                    act.activation(hidden[:, f, :], relu[:], ACT.Square).then_inc(hidden_ready, 1)
                elif step == "proj":
                    copy_out(drive[:], use)
                elif step == "network":
                    for k, f in enumerate(range(0, CHUNKS, 2)):
                        act.wait_ge(hidden_ready, n * CHUNKS + k)
                        act.wait_ge(fc_full, f + 1)
                        act.activation(relu[:], fc_banks[f][:], ACT.Relu).then_inc(relu_ready, 1)
                        act.wait_ge(relu_ready, k + 1)
                        act.activation(hidden[:, f, :], relu[:], ACT.Square).then_inc(hidden_ready, 1)
                    copy_out(drive[:], use)

            def setup(name):
                if name == "low_rank":
                    return
                act.wait_ge(misc_full, misc_at(("w." + name, 0), 0) + 1)
                q_order, k_order = "c (r a d) -> c d a r", "c (r a d) -> c a d r"

                def put(to, src, order=None, scale=1.0):
                    if order:
                        src = src.rearrange(order, a=2, d=HEAD_DIM)
                        a, b = (HEAD_DIM, 2) if order == q_order else (2, HEAD_DIM)
                        to = to.rearrange("c (x y r) -> c x y r", x=a, y=b)
                    return act.activation(to, src, ACT.Copy, scale=scale)

                if name == "weights_turned":
                    put(uq_t[:], misc[0:LATENT, 0:P])
                    put(o_t[:], misc[:, P:2 * P])
                    last = put(a_t[:], misc[0:RANK, 2 * P:3 * P])
                elif name == "weights_1":
                    put(wq[0][:], misc[:, 0:P], q_order, SCALE)
                    put(qk_t[:], misc[:, P:2 * P])
                    last = put(v_eff[:], misc[0:LATENT, 2 * P:3 * P])
                elif name == "weights_2":
                    put(k_eff_t[:], misc[0:LATENT, 0:P])
                    last = put(wv[0][:], misc[:, P:2 * P])
                elif name == "weights_3":
                    last = put(wk[0][:], misc[:, 0:P], k_order)
                elif name == "circulants":
                    put(wq[1][:], misc[:, 0:P], q_order, SCALE)
                    put(wk[1][:], misc[:, P:2 * P], k_order)
                    put(wv[1][:], misc[:, 2 * P:3 * P])
                    last = put(w_out[:], misc[:, 3 * P:4 * P])
                elif name == "bias_columns":
                    put(bias_q[:], misc[:, 0:1], scale=SCALE)
                    last = put(bias_k[:], misc[:, 1:2])
                elif name == "fc_turned":
                    last = put(fc_t[:], misc[:])
                elif name == "proj_turned":
                    last = put(proj_t[:].rearrange("p f c -> p (f c)"), misc[:])
                last.then_inc(misc_free, 1)

            act.sem_inc(tile_read, SCORE_BANKS)
            act.sem_inc(pv_done, P_RING)
            for step in START:
                side(*step, 0)
            take_max(0, 0)

            def slot(s, turn):
                tiles = range(len(tiles_of(s)))
                for t in tiles[:2]:
                    exp_tile(s, t, turn)
                if s % BLOCKS == 0 and s > 0:
                    take_heads(s // BLOCKS - 1, turn)
                for kind, group in early_misc(s):
                    if kind == "max":
                        take_max(group, turn)
                for step in SIDE_STEPS[s][0]:
                    side(*step, turn)
                for t in tiles[2:]:
                    exp_tile(s, t, turn)
                for step in SIDE_STEPS[s][1]:
                    side(*step, turn)

            for s in range(LOOP):
                slot(s, 0)
            with act.Fori(0, TURNS) as turn:
                for s in range(LOOP, LOOP_END):
                    slot(s, turn)
            for s in range(AFTER, SLOTS):
                slot(s, 0)
            take_heads(ALL_GROUPS - 1, 0)
            for step in E_LAST:
                side("e", step, BATCHES - 1, 0)


_INS = ['L0_attn_x', 'L0_attn_W_dq', 'L0_attn_W_uq', 'L0_attn_W_dkv', 'L0_attn_W_uk', 'L0_attn_W_uv', 'L0_attn_W_o',
        'L0_ffn_kernel', 'L0_ffn_bias', 'L0_ffn_a', 'L0_ffn_b',
        'L1_attn_wq_c', 'L1_attn_wq_b', 'L1_attn_wk_c', 'L1_attn_wk_b', 'L1_attn_wv_c', 'L1_attn_wv_b',
        'L1_attn_wo_c', 'L1_attn_wo_b', 'L1_ffn_W_fc', 'L1_ffn_W_proj']
_OUTS = [((BATCHES, TOKENS, DIM), 'float32')]


def kernel(**inputs):
    import numpy as _np
    import concourse.bacc as _bacc
    from concourse import mybir as _mybir
    from concourse.bass_utils import run_bass_kernel_spmd as _run

    nc = _bacc.Bacc("TRN2", target_bir_lowering=False, num_devices=1)
    arrays, args = {}, []
    for name in _INS:
        a = _np.ascontiguousarray(inputs[name])
        arrays[f"in_{name}_dram"] = a
        args.append(nc.dram_tensor(f"in_{name}_dram", a.shape, _mybir.dt.from_np(a.dtype), kind="ExternalInput").ap())
    for i, (shape, dtype) in enumerate(_OUTS):
        dt = _mybir.dt.from_np(_np.dtype(dtype))
        args.append(nc.dram_tensor(f"out_{i}_dram", shape, dt, kind="ExternalOutput").ap())
    build_program(nc, *args)
    r = _run(nc, [arrays], core_ids=[0])
    got = tuple(r.results[0][f"out_{i}_dram"] for i in range(len(_OUTS)))
    return got[0]
```
